# Optimizing a Trainium2 kernel written in Bass

```python
import numpy as np
import jax
import jax.numpy as jnp

def _softmax(x, axis=-1):
    return jax.nn.softmax(x, axis=axis)

def _gelu(x):
    return jax.nn.gelu(x, approximate=True)

def _silu(x):
    return jax.nn.silu(x)

def _sigmoid(x):
    return jax.nn.sigmoid(x)

def _layernorm(x, axis=-1, eps=1e-05):
    m = jnp.mean(x, axis=axis, keepdims=True)
    v = jnp.var(x, axis=axis, keepdims=True)
    return (x - m) / jnp.sqrt(v + eps)

def _scatter_add(tgt, idx, src, axis=0):
    return tgt.at[idx].add(src)

def _segment_sum(src, seg, n):
    return jax.ops.segment_sum(src, seg, n)
kernel_name = 'mk_hybrid_d1_jaxref_r8_0a9580'

def setup_inputs(seed: int=0):
    np.random.seed(seed)
    _w = jnp.asarray

    def _L0_attn_a_setup():
        import jax, jax.numpy as jnp
        import numpy as np
        B, S, DIM = (1, 256, 256)
        HEADS, KV_HEADS = (32, 8)
        DH = DIM // HEADS
        G = HEADS // KV_HEADS
        CBLK = 16
        SBLK = 16
        NSEL = 8
        WIN = 64
        SCALE = DH ** (-0.5)
        NEG = -1e+30
        CDIM = CBLK * DH

        def _rope(x, pos):
            d = x.shape[-1]
            inv = 1.0 / 10000.0 ** (jnp.arange(0, d, 2, dtype=jnp.float32) / d)
            ang = pos[:, None] * inv[None, :]
            cos, sin = (jnp.cos(ang), jnp.sin(ang))
            x1, x2 = (x[..., 0::2], x[..., 1::2])
            return jnp.stack([x1 * cos - x2 * sin, x1 * sin + x2 * cos], axis=-1).reshape(x.shape)

        def _forward(x, w_qkv, k_pos, v_pos, k_cw1, k_cb1, k_cw2, k_cb2, v_cw1, v_cb1, v_cw2, v_cb2, mem_ck, mem_cv, w_gate, b_gate, w_out):
            b, n, _ = x.shape
            di, dkv = (HEADS * DH, KV_HEADS * DH)
            qkv = x @ w_qkv
            q = qkv[..., :di].reshape(b, n, KV_HEADS, G, DH).transpose(0, 2, 3, 1, 4)
            k = qkv[..., di:di + dkv].reshape(b, n, KV_HEADS, DH).transpose(0, 2, 1, 3)
            v = qkv[..., di + dkv:].reshape(b, n, KV_HEADS, DH).transpose(0, 2, 1, 3)
            nc = n // CBLK
            kb = k[:, :, :nc * CBLK].reshape(b, KV_HEADS, nc, CBLK, DH) + k_pos[None, :, None]
            vb = v[:, :, :nc * CBLK].reshape(b, KV_HEADS, nc, CBLK, DH) + v_pos[None, :, None]
            ck = jax.nn.relu(kb.reshape(b, KV_HEADS, nc, CDIM) @ k_cw1 + k_cb1) @ k_cw2 + k_cb2
            cv = jax.nn.relu(vb.reshape(b, KV_HEADS, nc, CDIM) @ v_cw1 + v_cb1) @ v_cw2 + v_cb2
            ck = jnp.concatenate([jnp.broadcast_to(mem_ck[None], (b, KV_HEADS, 1, DH)), ck], axis=2)
            cv = jnp.concatenate([jnp.broadcast_to(mem_cv[None], (b, KV_HEADS, 1, DH)), cv], axis=2)
            csim = jnp.einsum('bhgnd,bhjd->bhgnj', q, ck) * SCALE
            ck_last = jnp.concatenate([jnp.array([-1]), (jnp.arange(nc) + 1) * CBLK - 1])
            cmask = ck_last[None, :] < jnp.arange(n)[:, None]
            csim = jnp.where(cmask, csim, NEG)
            c_out = jnp.einsum('bhgnj,bhjd->bhgnd', jax.nn.softmax(csim, -1), cv)
            imp = csim[..., 1:].mean(axis=2)
            imp = jnp.concatenate([jnp.full(imp.shape[:-1] + (1,), -1000.0, imp.dtype), imp], axis=-1)
            imp = jax.nn.softmax(imp, -1)[..., 1:]
            sel_vals, sel_idx = jax.lax.top_k(imp, NSEL)
            fine_gate_mask = sel_vals > 1e-10
            pos = jnp.arange(n, dtype=jnp.float32)
            rq, rk = (_rope(q, pos), _rope(k, pos))
            nf = n // SBLK
            own = jnp.broadcast_to((jnp.arange(n) // SBLK)[None, None, :, None], (b, KV_HEADS, n, 1))
            idx = jnp.concatenate([sel_idx, own], axis=-1)
            kblocks = rk.reshape(b, KV_HEADS, nf, SBLK, DH)
            vblocks = v.reshape(b, KV_HEADS, nf, SBLK, DH)
            bi = jnp.arange(b)[:, None, None, None]
            hi = jnp.arange(KV_HEADS)[None, :, None, None]
            fk = kblocks[bi, hi, idx].reshape(b, KV_HEADS, n, (NSEL + 1) * SBLK, DH)
            fv = vblocks[bi, hi, idx].reshape(b, KV_HEADS, n, (NSEL + 1) * SBLK, DH)
            sel_m = jnp.repeat(fine_gate_mask[..., None], SBLK, -1).reshape(b, KV_HEADS, n, NSEL * SBLK)
            diag_m = (jnp.arange(n) % SBLK)[:, None] >= jnp.arange(SBLK)[None, :]
            fmask = jnp.concatenate([sel_m, jnp.broadcast_to(diag_m[None, None], (b, KV_HEADS, n, SBLK))], axis=-1)
            fsim = jnp.einsum('bhgnd,bhnjd->bhgnj', rq, fk) * SCALE
            fsim = jnp.where(fmask[:, :, None], fsim, NEG)
            f_out = jnp.einsum('bhgnj,bhnjd->bhgnd', jax.nn.softmax(fsim, -1), fv)
            nwin = n // WIN
            qw = rq.reshape(b, KV_HEADS, G, nwin, WIN, DH)
            kw = rk.reshape(b, KV_HEADS, nwin, WIN, DH)
            vw = v.reshape(b, KV_HEADS, nwin, WIN, DH)
            kcat = jnp.concatenate([jnp.concatenate([jnp.zeros_like(kw[:, :, :1]), kw[:, :, :-1]], 2), kw], 3)
            vcat = jnp.concatenate([jnp.concatenate([jnp.zeros_like(vw[:, :, :1]), vw[:, :, :-1]], 2), vw], 3)
            ssim = jnp.einsum('bhgwid,bhwjd->bhgwij', qw, kcat) * SCALE
            i_, j_ = (jnp.arange(WIN), jnp.arange(2 * WIN))
            delta = i_[:, None] - (j_[None, :] - WIN)
            smask = ((delta >= 0) & (delta <= WIN))[None] & ((jnp.arange(nwin) > 0)[:, None, None] | (j_ >= WIN)[None, None, :])
            ssim = jnp.where(smask[None, None, None], ssim, NEG)
            s_out = jnp.einsum('bhgwij,bhwjd->bhgwid', jax.nn.softmax(ssim, -1), vcat)
            s_out = s_out.reshape(b, KV_HEADS, G, n, DH)
            gates = jax.nn.sigmoid(x @ w_gate + b_gate).reshape(b, n, KV_HEADS, G, 3).transpose(0, 2, 3, 1, 4)
            out = gates[..., 0:1] * c_out + gates[..., 1:2] * f_out + gates[..., 2:3] * s_out
            out = out.transpose(0, 3, 1, 2, 4).reshape(b, n, HEADS * DH)
            return out @ w_out
        key = jax.random.key(seed)
        ks = jax.random.split(key, 16)

        def rnd(i, shape, sc=0.02):
            return jax.random.normal(ks[i], shape, dtype=jnp.float32) * sc
        dim_inner, dim_kv = (HEADS * DH, KV_HEADS * DH)
        return {'hidden_states': jax.random.normal(ks[0], (B, S, DIM), dtype=jnp.float32), 'w_qkv': rnd(1, (DIM, dim_inner + 2 * dim_kv)), 'k_pos': rnd(2, (KV_HEADS, CBLK, DH)), 'v_pos': rnd(3, (KV_HEADS, CBLK, DH)), 'k_cw1': rnd(4, (CDIM, CDIM)), 'k_cb1': jnp.zeros((CDIM,), jnp.float32), 'k_cw2': rnd(5, (CDIM, DH)), 'k_cb2': jnp.zeros((DH,), jnp.float32), 'v_cw1': rnd(6, (CDIM, CDIM)), 'v_cb1': jnp.zeros((CDIM,), jnp.float32), 'v_cw2': rnd(7, (CDIM, DH)), 'v_cb2': jnp.zeros((DH,), jnp.float32), 'mem_ck': rnd(8, (KV_HEADS, 1, DH)), 'mem_cv': rnd(9, (KV_HEADS, 1, DH)), 'w_gate': rnd(10, (DIM, 3 * HEADS)), 'b_gate': jnp.tile(jnp.array([-2.0, -2.0, 2.0], jnp.float32), HEADS), 'w_out': rnd(11, (dim_inner, DIM))}
    _L0_attn_a_in = _L0_attn_a_setup()

    def _L0_attn_b_setup():
        import jax, jax.numpy as jnp
        import numpy as np
        DIM = 256
        N_HEADS = 16
        N_KV_HEADS = 4
        WINDOW = 64
        GLOBAL = 64

        def alibi_slopes(num_heads):
            closest_pow2 = 2.0 ** np.floor(np.log2(num_heads))
            base = 2.0 ** (-2.0 ** (-(np.log2(closest_pow2) - 3.0)))
            powers = np.arange(1, 1 + num_heads, dtype=np.float32)
            return jnp.asarray(base ** powers, dtype=jnp.float32)

        def window_allowed(seq_len):
            i = jnp.arange(seq_len)[:, None]
            j = jnp.arange(seq_len)[None, :]
            inside = (j >= i - WINDOW // 2) & (j <= i + WINDOW // 2)
            glob = (i < GLOBAL) | (j < GLOBAL)
            return inside | glob
        key = jax.random.key(seed)
        k1, k2, k3, k4 = jax.random.split(key, 4)
        B, S, D = (2, 256, DIM)
        kv_feat = 2 * D * N_KV_HEADS // N_HEADS
        std = 0.02
        x = jax.random.normal(k1, (B, S, D), dtype=jnp.float32)
        Wq = jax.random.normal(k2, (D, D), dtype=jnp.float32) * std
        Wkv = jax.random.normal(k3, (D, kv_feat), dtype=jnp.float32) * std
        Wo = jax.random.normal(k4, (D, D), dtype=jnp.float32) * std
        bo = jnp.zeros((D,), dtype=jnp.float32)
        return {'x': x, 'Wq': Wq, 'Wkv': Wkv, 'Wo': Wo, 'bo': bo}
    _L0_attn_b_in = _L0_attn_b_setup()

    def _L0_ffn_setup():
        import jax, jax.numpy as jnp
        import numpy as np
        B, S, D, H = (8, 512, 256, 640)

        def ternarize_weight(w):
            abs_mean = jnp.maximum(jnp.mean(jnp.abs(w)), 1e-05)
            thr = 0.7 * abs_mean
            one = jnp.ones((), dtype=w.dtype)
            q = jnp.where(w > thr, one, jnp.where(w < -thr, -one, jnp.zeros((), dtype=w.dtype)))
            return w + jax.lax.stop_gradient(q * abs_mean - w)
        key = jax.random.key(seed)
        k1, k2, k3 = jax.random.split(key, 3)
        x = jax.random.normal(k1, (B, S, D), dtype=jnp.float32)
        w_fc = jax.random.normal(k2, (H, D), dtype=jnp.float32) / np.sqrt(D).astype(np.float32)
        w_proj = jax.random.normal(k3, (D, H), dtype=jnp.float32) / np.sqrt(H).astype(np.float32)
        return {'x': x, 'w_fc': w_fc, 'w_proj': w_proj}
    _L0_ffn_in = _L0_ffn_setup()
    _d = {'L0_attn_a_hidden_states': _L0_attn_a_in['hidden_states'], 'L0_attn_a_w_qkv': _L0_attn_a_in['w_qkv'], 'L0_attn_a_k_pos': _L0_attn_a_in['k_pos'], 'L0_attn_a_v_pos': _L0_attn_a_in['v_pos'], 'L0_attn_a_k_cw1': _L0_attn_a_in['k_cw1'], 'L0_attn_a_k_cb1': _L0_attn_a_in['k_cb1'], 'L0_attn_a_k_cw2': _L0_attn_a_in['k_cw2'], 'L0_attn_a_k_cb2': _L0_attn_a_in['k_cb2'], 'L0_attn_a_v_cw1': _L0_attn_a_in['v_cw1'], 'L0_attn_a_v_cb1': _L0_attn_a_in['v_cb1'], 'L0_attn_a_v_cw2': _L0_attn_a_in['v_cw2'], 'L0_attn_a_v_cb2': _L0_attn_a_in['v_cb2'], 'L0_attn_a_mem_ck': _L0_attn_a_in['mem_ck'], 'L0_attn_a_mem_cv': _L0_attn_a_in['mem_cv'], 'L0_attn_a_w_gate': _L0_attn_a_in['w_gate'], 'L0_attn_a_b_gate': _L0_attn_a_in['b_gate'], 'L0_attn_a_w_out': _L0_attn_a_in['w_out'], 'L0_attn_b_Wq': _L0_attn_b_in['Wq'], 'L0_attn_b_Wkv': _L0_attn_b_in['Wkv'], 'L0_attn_b_Wo': _L0_attn_b_in['Wo'], 'L0_attn_b_bo': _L0_attn_b_in['bo'], 'L0_ffn_w_fc': _L0_ffn_in['w_fc'], 'L0_ffn_w_proj': _L0_ffn_in['w_proj']}
    _x0 = _d['L0_attn_a_hidden_states']
    _d['L0_attn_a_hidden_states'] = jax.random.normal(jax.random.fold_in(jax.random.key(seed), 1), (4, 1024, 256), dtype=_x0.dtype)
    del _x0
    return _d

def reference(L0_attn_a_hidden_states, L0_attn_a_w_qkv, L0_attn_a_k_pos, L0_attn_a_v_pos, L0_attn_a_k_cw1, L0_attn_a_k_cb1, L0_attn_a_k_cw2, L0_attn_a_k_cb2, L0_attn_a_v_cw1, L0_attn_a_v_cb1, L0_attn_a_v_cw2, L0_attn_a_v_cb2, L0_attn_a_mem_ck, L0_attn_a_mem_cv, L0_attn_a_w_gate, L0_attn_a_b_gate, L0_attn_a_w_out, L0_attn_b_Wq, L0_attn_b_Wkv, L0_attn_b_Wo, L0_attn_b_bo, L0_ffn_w_fc, L0_ffn_w_proj):

    def _L0_attn_a_ref(hidden_states, w_qkv, k_pos, v_pos, k_cw1, k_cb1, k_cw2, k_cb2, v_cw1, v_cb1, v_cw2, v_cb2, mem_ck, mem_cv, w_gate, b_gate, w_out):
        import jax, jax.numpy as jnp
        import numpy as np
        B, S, DIM = (1, 256, 256)
        HEADS, KV_HEADS = (32, 8)
        DH = DIM // HEADS
        G = HEADS // KV_HEADS
        CBLK = 16
        SBLK = 16
        NSEL = 8
        WIN = 64
        SCALE = DH ** (-0.5)
        NEG = -1e+30
        CDIM = CBLK * DH

        def _rope(x, pos):
            d = x.shape[-1]
            inv = 1.0 / 10000.0 ** (jnp.arange(0, d, 2, dtype=jnp.float32) / d)
            ang = pos[:, None] * inv[None, :]
            cos, sin = (jnp.cos(ang), jnp.sin(ang))
            x1, x2 = (x[..., 0::2], x[..., 1::2])
            return jnp.stack([x1 * cos - x2 * sin, x1 * sin + x2 * cos], axis=-1).reshape(x.shape)

        def _forward(x, w_qkv, k_pos, v_pos, k_cw1, k_cb1, k_cw2, k_cb2, v_cw1, v_cb1, v_cw2, v_cb2, mem_ck, mem_cv, w_gate, b_gate, w_out):
            b, n, _ = x.shape
            di, dkv = (HEADS * DH, KV_HEADS * DH)
            qkv = x @ w_qkv
            q = qkv[..., :di].reshape(b, n, KV_HEADS, G, DH).transpose(0, 2, 3, 1, 4)
            k = qkv[..., di:di + dkv].reshape(b, n, KV_HEADS, DH).transpose(0, 2, 1, 3)
            v = qkv[..., di + dkv:].reshape(b, n, KV_HEADS, DH).transpose(0, 2, 1, 3)
            nc = n // CBLK
            kb = k[:, :, :nc * CBLK].reshape(b, KV_HEADS, nc, CBLK, DH) + k_pos[None, :, None]
            vb = v[:, :, :nc * CBLK].reshape(b, KV_HEADS, nc, CBLK, DH) + v_pos[None, :, None]
            ck = jax.nn.relu(kb.reshape(b, KV_HEADS, nc, CDIM) @ k_cw1 + k_cb1) @ k_cw2 + k_cb2
            cv = jax.nn.relu(vb.reshape(b, KV_HEADS, nc, CDIM) @ v_cw1 + v_cb1) @ v_cw2 + v_cb2
            ck = jnp.concatenate([jnp.broadcast_to(mem_ck[None], (b, KV_HEADS, 1, DH)), ck], axis=2)
            cv = jnp.concatenate([jnp.broadcast_to(mem_cv[None], (b, KV_HEADS, 1, DH)), cv], axis=2)
            csim = jnp.einsum('bhgnd,bhjd->bhgnj', q, ck) * SCALE
            ck_last = jnp.concatenate([jnp.array([-1]), (jnp.arange(nc) + 1) * CBLK - 1])
            cmask = ck_last[None, :] < jnp.arange(n)[:, None]
            csim = jnp.where(cmask, csim, NEG)
            c_out = jnp.einsum('bhgnj,bhjd->bhgnd', jax.nn.softmax(csim, -1), cv)
            imp = csim[..., 1:].mean(axis=2)
            imp = jnp.concatenate([jnp.full(imp.shape[:-1] + (1,), -1000.0, imp.dtype), imp], axis=-1)
            imp = jax.nn.softmax(imp, -1)[..., 1:]
            sel_vals, sel_idx = jax.lax.top_k(imp, NSEL)
            fine_gate_mask = sel_vals > 1e-10
            pos = jnp.arange(n, dtype=jnp.float32)
            rq, rk = (_rope(q, pos), _rope(k, pos))
            nf = n // SBLK
            own = jnp.broadcast_to((jnp.arange(n) // SBLK)[None, None, :, None], (b, KV_HEADS, n, 1))
            idx = jnp.concatenate([sel_idx, own], axis=-1)
            kblocks = rk.reshape(b, KV_HEADS, nf, SBLK, DH)
            vblocks = v.reshape(b, KV_HEADS, nf, SBLK, DH)
            bi = jnp.arange(b)[:, None, None, None]
            hi = jnp.arange(KV_HEADS)[None, :, None, None]
            fk = kblocks[bi, hi, idx].reshape(b, KV_HEADS, n, (NSEL + 1) * SBLK, DH)
            fv = vblocks[bi, hi, idx].reshape(b, KV_HEADS, n, (NSEL + 1) * SBLK, DH)
            sel_m = jnp.repeat(fine_gate_mask[..., None], SBLK, -1).reshape(b, KV_HEADS, n, NSEL * SBLK)
            diag_m = (jnp.arange(n) % SBLK)[:, None] >= jnp.arange(SBLK)[None, :]
            fmask = jnp.concatenate([sel_m, jnp.broadcast_to(diag_m[None, None], (b, KV_HEADS, n, SBLK))], axis=-1)
            fsim = jnp.einsum('bhgnd,bhnjd->bhgnj', rq, fk) * SCALE
            fsim = jnp.where(fmask[:, :, None], fsim, NEG)
            f_out = jnp.einsum('bhgnj,bhnjd->bhgnd', jax.nn.softmax(fsim, -1), fv)
            nwin = n // WIN
            qw = rq.reshape(b, KV_HEADS, G, nwin, WIN, DH)
            kw = rk.reshape(b, KV_HEADS, nwin, WIN, DH)
            vw = v.reshape(b, KV_HEADS, nwin, WIN, DH)
            kcat = jnp.concatenate([jnp.concatenate([jnp.zeros_like(kw[:, :, :1]), kw[:, :, :-1]], 2), kw], 3)
            vcat = jnp.concatenate([jnp.concatenate([jnp.zeros_like(vw[:, :, :1]), vw[:, :, :-1]], 2), vw], 3)
            ssim = jnp.einsum('bhgwid,bhwjd->bhgwij', qw, kcat) * SCALE
            i_, j_ = (jnp.arange(WIN), jnp.arange(2 * WIN))
            delta = i_[:, None] - (j_[None, :] - WIN)
            smask = ((delta >= 0) & (delta <= WIN))[None] & ((jnp.arange(nwin) > 0)[:, None, None] | (j_ >= WIN)[None, None, :])
            ssim = jnp.where(smask[None, None, None], ssim, NEG)
            s_out = jnp.einsum('bhgwij,bhwjd->bhgwid', jax.nn.softmax(ssim, -1), vcat)
            s_out = s_out.reshape(b, KV_HEADS, G, n, DH)
            gates = jax.nn.sigmoid(x @ w_gate + b_gate).reshape(b, n, KV_HEADS, G, 3).transpose(0, 2, 3, 1, 4)
            out = gates[..., 0:1] * c_out + gates[..., 1:2] * f_out + gates[..., 2:3] * s_out
            out = out.transpose(0, 3, 1, 2, 4).reshape(b, n, HEADS * DH)
            return out @ w_out
        return _forward(hidden_states, w_qkv, k_pos, v_pos, k_cw1, k_cb1, k_cw2, k_cb2, v_cw1, v_cb1, v_cw2, v_cb2, mem_ck, mem_cv, w_gate, b_gate, w_out)

    def _L0_attn_b_ref(x, Wq, Wkv, Wo, bo):
        import jax, jax.numpy as jnp
        import numpy as np
        DIM = 256
        N_HEADS = 16
        N_KV_HEADS = 4
        WINDOW = 64
        GLOBAL = 64

        def alibi_slopes(num_heads):
            closest_pow2 = 2.0 ** np.floor(np.log2(num_heads))
            base = 2.0 ** (-2.0 ** (-(np.log2(closest_pow2) - 3.0)))
            powers = np.arange(1, 1 + num_heads, dtype=np.float32)
            return jnp.asarray(base ** powers, dtype=jnp.float32)

        def window_allowed(seq_len):
            i = jnp.arange(seq_len)[:, None]
            j = jnp.arange(seq_len)[None, :]
            inside = (j >= i - WINDOW // 2) & (j <= i + WINDOW // 2)
            glob = (i < GLOBAL) | (j < GLOBAL)
            return inside | glob
        B, S, D = x.shape
        H, KVH = (N_HEADS, N_KV_HEADS)
        hd = D // H
        r = H // KVH
        cw = jax.nn.sigmoid(jnp.sum(jnp.abs(x), axis=-1, keepdims=True))
        q = jnp.dot(x * cw, Wq)
        kv = jnp.dot(x, Wkv)
        k, v = jnp.split(kv, 2, axis=-1)
        q = q.reshape(B, S, H, hd).transpose(0, 2, 1, 3)
        k = k.reshape(B, S, KVH, hd).transpose(0, 2, 1, 3)
        v = v.reshape(B, S, KVH, hd).transpose(0, 2, 1, 3)
        k = jnp.repeat(k, r, axis=1)
        v = jnp.repeat(v, r, axis=1)
        scale = 1.0 / jnp.sqrt(jnp.float32(hd))
        qk = jnp.einsum('bhid,bhjd->bhij', q, k) * scale
        pos = jnp.arange(S)
        dist = -jnp.abs(pos[:, None] - pos[None, :]).astype(jnp.float32)
        qk = qk + alibi_slopes(H)[None, :, None, None] * dist[None, None, :, :]
        allowed = window_allowed(S)
        qk = jnp.where(allowed[None, None, :, :], -1000000000.0, qk)
        attn = jax.nn.softmax(qk, axis=-1)
        out = jnp.einsum('bhij,bhjd->bhid', attn, v)
        out = out.transpose(0, 2, 1, 3).reshape(B, S, D)
        return jnp.dot(out, Wo) + bo

    def _L0_ffn_ref(x, w_fc, w_proj):
        import jax, jax.numpy as jnp
        import numpy as np
        B, S, D, H = (8, 512, 256, 640)

        def ternarize_weight(w):
            abs_mean = jnp.maximum(jnp.mean(jnp.abs(w)), 1e-05)
            thr = 0.7 * abs_mean
            one = jnp.ones((), dtype=w.dtype)
            q = jnp.where(w > thr, one, jnp.where(w < -thr, -one, jnp.zeros((), dtype=w.dtype)))
            return w + jax.lax.stop_gradient(q * abs_mean - w)
        h = jnp.einsum('bsd,hd->bsh', x, ternarize_weight(w_fc))
        h = jnp.square(jax.nn.relu(h))
        return jnp.einsum('bsh,dh->bsd', h, ternarize_weight(w_proj))
    x = L0_attn_a_hidden_states
    x = x + _L0_attn_a_ref(_layernorm(x, axis=-1), L0_attn_a_w_qkv, L0_attn_a_k_pos, L0_attn_a_v_pos, L0_attn_a_k_cw1, L0_attn_a_k_cb1, L0_attn_a_k_cw2, L0_attn_a_k_cb2, L0_attn_a_v_cw1, L0_attn_a_v_cb1, L0_attn_a_v_cw2, L0_attn_a_v_cb2, L0_attn_a_mem_ck, L0_attn_a_mem_cv, L0_attn_a_w_gate, L0_attn_a_b_gate, L0_attn_a_w_out)
    x = x + _L0_ffn_ref(_layernorm(x, axis=-1), L0_ffn_w_fc, L0_ffn_w_proj)
    x = x + _L0_attn_b_ref(_layernorm(x, axis=-1), L0_attn_b_Wq, L0_attn_b_Wkv, L0_attn_b_Wo, L0_attn_b_bo)
    x = x + _L0_ffn_ref(_layernorm(x, axis=-1), L0_ffn_w_fc, L0_ffn_w_proj)
    return x

_drawn_inputs = setup_inputs


def setup_inputs(seed=0):
    import zlib

    import numpy as np

    out = dict(_drawn_inputs(seed))
    spreads = {'L0_attn_a_k_cb1': (0.0, 0.8),
     'L0_attn_a_k_cb2': (0.0, 0.8),
     'L0_attn_a_v_cb1': (0.0, 0.8),
     'L0_attn_a_v_cb2': (0.0, 0.8),
     'L0_attn_b_bo': (0.0, 0.1)}
    factors = {'L0_attn_a_w_qkv': 5.436,
     'L0_attn_a_k_pos': 8.0,
     'L0_attn_a_v_pos': 8.0,
     'L0_attn_a_k_cw1': 8.0,
     'L0_attn_a_k_cw2': 8.0,
     'L0_attn_a_v_cw1': 8.0,
     'L0_attn_a_v_cw2': 8.0,
     'L0_attn_a_mem_ck': 58.667,
     'L0_attn_a_mem_cv': 61.266,
     'L0_attn_a_w_gate': 8.0,
     'L0_attn_a_w_out': 5.254,
     'L0_attn_b_Wq': 8.0,
     'L0_attn_b_Wkv': 3.576,
     'L0_attn_b_Wo': 3.443}
    for name, (base, spread) in spreads.items():
        noise = np.random.default_rng([zlib.crc32(name.encode()), seed]).standard_normal(out[name].shape)
        drawn = base * np.exp(spread * noise) if base else spread * noise
        out[name] = jnp.asarray(drawn.astype(out[name].dtype))
    for name, factor in factors.items():
        out[name] = (out[name] * factor).astype(out[name].dtype)
    return out
```

```python
import concourse.bass as bass
from concourse import mybir
from concourse.alu_op_type import AluOpType as ALU
from contextlib import ExitStack

F32 = mybir.dt.float32
BF16 = mybir.dt.bfloat16
ACT = mybir.ActivationFunctionType
AX = mybir.AxisListType.X

B, N, D = 4, 1024, 256
P = 128
TILES = B * N // P
QT = N // P
EPS = 1e-5
NEG = -2.0 ** 60

HA, GA, DA = 8, 4, 8
BLK, NBLK, NSEL, WIN = 16, 64, 8, 64
UA = B * HA
SCALE_A = float(DA) ** -0.5
HB, GB, DB = 4, 4, 16
UB = B * HB
SCALE_B = float(DB) ** -0.5
HID = 640
GRP = 512
NG = B * N // GRP

TOKC = 96 + 64 + 64


class Steps:

    def __init__(self, sem, names):
        self.sem, self.names, self.n = sem, list(names), len(names)

    def at(self, rnd, name):
        return rnd * self.n + (self.names.index(name) + 1)


def wait(eng, sem, value):
    if isinstance(value, int) and value <= 0:
        return
    eng.wait_ge(sem, value)


class Mem:

    def __init__(self, nc, ctx):
        self.nc, self.ctx = nc, ctx

    def sb(self, name, shape, dt=F32):
        return self.ctx.enter_context(self.nc.sbuf_tensor(name, shape, dt))

    def ps(self, name):
        return self.ctx.enter_context(self.nc.psum_tensor(name, [P, 8, 512], F32))

    def sem(self, name):
        return self.ctx.enter_context(self.nc.semaphore(name))


def rows(ap, offset, dims):
    return bass.AP(ap.tensor, offset, [list(d) for d in dims])


NEWTON = ("vr", "vrr", "half", "r")


def newton(nc, step, r, v, t):
    if step == "vr":
        return nc.vector.tensor_tensor(t, v, r, ALU.mult)
    if step == "vrr":
        return nc.vector.tensor_tensor(t, t, r, ALU.mult)
    if step == "half":
        return nc.vector.tensor_scalar(t, t, -0.5, 1.5, ALU.mult, ALU.add)
    return nc.vector.tensor_tensor(r, r, t, ALU.mult)


def project_a(nc, sems, G, I, S):
    with ExitStack() as ctx:
        m = Mem(nc, ctx)
        wq = m.sb("wq", [P, 2, 2, 256])
        wk = m.sb("wk", [P, 2, 2, 64])
        wt = m.sb("wt", [P, 2, TOKC])
        rope_q = m.sb("rope_q", [P, 2, N])
        rope_k = m.sb("rope_k", [64, 2, N])
        bgate = m.sb("bgate", [P, 96])
        stat = m.sb("p1_stat", [P, TILES, 6])
        mv = m.sb("p1_mv", [P, TILES, 2])
        rstd = m.sb("p1_rstd", [P, TILES])
        var = m.sb("p1_var", [P, TILES])
        scr = m.sb("p1_scratch", [P, TILES])
        xn = m.sb("p1_xn", [P, 2, 4, D])
        xnT = m.sb("p1_xnT", [P, 2, 2, GRP])
        split = m.sb("p1_split", [P, 2, 2, 6, GRP], BF16)
        ksplit = m.sb("p1_ksplit", [64, 2, 3, GRP], BF16)
        qres = m.sb("p1_qres", [P, 2, 2, GRP])
        tcos = m.sb("p1_tcos", [P, 2, 2, GRP])
        tsin = m.sb("p1_tsin", [P, 2, 2, GRP])
        rres = m.sb("p1_rres", [P, 2, 2, GRP])
        kcos = m.sb("p1_kcos", [64, 2, GRP])
        ksin = m.sb("p1_ksin", [64, 2, GRP])
        kres = m.sb("p1_kres", [64, 2, GRP])
        vk = m.sb("p1_vk", [P, 2, 4, P])
        psum = m.ps("p1_psum")
        X, GT, VT, ident = G["X"], G["GT"], G["VT"], G["ident"]

        s_w = sems("p1_weights_loaded")
        s_x = [sems(f"p1_x_loaded{i}") for i in range(4)]
        s_ln = sems("p1_ln_steps")
        s_sq = sems("p1_std_ready")
        pe = Steps(sems("p1_pe_slot_ready"), ["T0", "T1", "Q0", "S0", "K", "Q1", "S1", "KS", "TM0", "TM1"])
        act = Steps(sems("p1_act_steps"), ["T0", "T1", "qh0", "qm0", "qh1", "qm1", "rh0", "rm0", "rh1", "rm1",
                                           "kh", "km", "tm0", "tm1"])
        dve = Steps(sems("p1_dve_steps"), ["c0", "e0", "s0", "l0", "ck", "c1", "e1", "s1", "l1", "sk",
                                           "g0", "g1", "g2", "g3"])
        pool = Steps(sems("p1_pool_steps"), ["rq0", "re0", "rl0", "rq1", "re1", "rl1", "rk", "rke", "rkl", "vt"])
        s_xn = sems("p1_xn_ready")
        s_wr = [sems(f"p1_scratch_written{i}") for i in range(2)]
        s_gate = sems("p1_gate_steps")
        s_vs = sems("p1_shifted_values")

        freed_by = {"T0": (dve, "e1", -1), "T1": (dve, "s1", -1), "Q0": (dve, "sk", -1), "S0": (dve, "g1", -1),
                    "K": (dve, "g3", -1), "Q1": (act, "T0", 0), "S1": (act, "T1", 0), "KS": (dve, "e0", 0),
                    "TM0": (dve, "s0", 0), "TM1": (dve, "ck", 0)}

        def bank(name):
            return psum[:, pe.names.index(name) % 5, :]

        def groups(body):
            def run(eng):
                body(eng, 0)
                with eng.Fori(1, B - 1) as b:
                    body(eng, b)
                body(eng, B - 1)
            return run

        with nc.Block() as block:
            @block.sync
            def _(sp):
                for i in range(4):
                    sp.dma_start(X[:, 8 * i:8 * i + 8, :], I["x"][1024 * i:1024 * i + 1024, :]
                                 .rearrange("(t p) c -> p t c", p=P)).then_inc(s_x[i], 16)
                for dst, src in ((ident, I["ident"]), (wq[:, 0], I["w_q"][0:P]), (wq[:, 1], I["w_q"][P:2 * P]),
                                 (wk[:, 0], I["w_k"][0:P]), (wk[:, 1], I["w_k"][P:2 * P]),
                                 (wt[:, 0], I["w_tok"][0:P]), (wt[:, 1], I["w_tok"][P:2 * P]),
                                 (rope_q, I["rope_q"]), (rope_k, I["rope_k"]),
                                 (bgate, rows(I["b_gate"], 0, [(0, P), (1, 96)]))):
                    sp.dma_start(dst[:] if not isinstance(dst, bass.AP) else dst, src[:]).then_inc(s_w, 16)

                def body(sp, b):
                    for half in range(2):
                        n = 2 * b + half
                        col = half * GRP
                        for f in range(2):
                            sp.wait_ge(pool.sem, pool.at(n, f"rl{f}"))
                            sp.dma_start(S["qd"][:, bass.ds(b, 1), f * P:f * P + P, col:col + GRP]
                                         .rearrange("s b p t -> p (b s) t"), split[:, half, f]).then_inc(s_wr[half], 16)
                        sp.wait_ge(pool.sem, pool.at(n, "rkl"))
                        sp.dma_start(S["kd"][:, bass.ds(b, 1), :, col:col + GRP].rearrange("s b p t -> p (b s) t"),
                                     ksplit[:, half]).then_inc(s_wr[half], 16)
                        sp.wait_ge(act.sem, act.at(n, "tm1"))
                        sp.dma_start(S["vkd"][bass.ds(b * N + col, GRP), :].rearrange("(t p) c -> p t c", p=P),
                                     vk[:, half]).then_inc(s_wr[half], 16)
                groups(body)(sp)
                for half in range(2):
                    sp.wait_ge(s_wr[half], 4 * B * 16)
                sp.wait_ge(pool.sem, pool.at(NG - 1, "vt"))
                vt = VT[:].rearrange("p b h t d -> p (b h) t d")
                vs = G["VS"][:].rearrange("p b h t d -> p (b h) t d")
                sp.dma_start(vs[64:P], vt[0:64]).then_inc(s_vs, 16)
                for t in range(1, QT):
                    sp.dma_start(vs[0:64, :, t, :], vt[64:P, :, t - 1, :]).then_inc(s_vs, 16)
                sp.wait_ge(s_vs, 16 * QT)

            @block.tensor
            def _(te):
                te.wait_ge(s_w, 160)

                def body(te, b):
                    for half in range(2):
                        n = 2 * b + half

                        def free(name):
                            by, step, back = freed_by[name]
                            wait(te, by.sem, by.at(n + back, step))

                        for k in range(2):
                            te.wait_ge(s_xn, 4 * (n + 1))
                            free(f"T{k}")
                            for j in range(4):
                                last = nc.tensor.transpose(bank(f"T{k}")[:, P * j:P * j + P],
                                                           xn[:, half, j, P * k:P * k + P], ident[:])
                            last.then_inc(pe.sem, 1)
                        te.wait_ge(act.sem, act.at(n, "T1"))
                        for name in ("Q0", "S0", "K", "Q1", "S1", "KS"):
                            free(name)
                            swap = name in ("S0", "S1", "KS")
                            for k in range(2):
                                w = wk[:, k, int(swap), :] if "K" in name else \
                                    wq[:, k, int(swap), P * int(name[1]):P * int(name[1]) + P]
                                out = bank(name)[0:64] if "K" in name else bank(name)
                                last = nc.tensor.matmul(out, w, xnT[:, half, k, :], start=(k == 0), stop=(k == 1))
                            last.then_inc(pe.sem, 1)
                        for i in range(2):
                            free(f"TM{i}")
                            for j in range(2):
                                row = P * (2 * i + j)
                                for k in range(2):
                                    last = nc.tensor.matmul(bank(f"TM{i}")[:, TOKC * j:TOKC * j + TOKC],
                                                            xnT[:, half, k, row:row + P], wt[:, k, :],
                                                            start=(k == 0), stop=(k == 1))
                            last.then_inc(pe.sem, 1)
                groups(body)(te)

            @block.scalar
            def _(sc):
                sc.wait_ge(s_ln, 2 * TILES + 1)
                nc.scalar.activation(rstd[:], var[:], ACT.Sqrt).then_inc(s_sq, 1)

                def body(sc, b):
                    for half in range(2):
                        n = 2 * b + half
                        for k in range(2):
                            sc.wait_ge(pe.sem, pe.at(n, f"T{k}"))
                            if k == 0:
                                wait(sc, pe.sem, pe.at(n - 2, "TM1"))
                            nc.scalar.copy(xnT[:, half, k, :], bank(f"T{k}")).then_inc(act.sem, 1)
                        wait(sc, s_wr[half], 64 * b)
                        for f in range(2):
                            sc.wait_ge(pe.sem, pe.at(n, f"Q{f}"))
                            nc.scalar.copy(split[:, half, f, 0, :], bank(f"Q{f}")).then_inc(act.sem, 1)
                            sc.wait_ge(dve.sem, dve.at(n, f"e{f}"))
                            nc.scalar.copy(split[:, half, f, 1, :], qres[:, half, f, :]).then_inc(act.sem, 1)
                        for f in range(2):
                            sc.wait_ge(pool.sem, pool.at(n, f"rq{f}"))
                            nc.scalar.copy(split[:, half, f, 3, :], tcos[:, half, f, :]).then_inc(act.sem, 1)
                            sc.wait_ge(pool.sem, pool.at(n, f"re{f}"))
                            nc.scalar.copy(split[:, half, f, 4, :], rres[:, half, f, :]).then_inc(act.sem, 1)
                        sc.wait_ge(pool.sem, pool.at(n, "rk"))
                        nc.scalar.copy(ksplit[:, half, 0, :], kcos[:, half, :]).then_inc(act.sem, 1)
                        sc.wait_ge(pool.sem, pool.at(n, "rke"))
                        nc.scalar.copy(ksplit[:, half, 1, :], kres[:, half, :]).then_inc(act.sem, 1)
                        for i in range(2):
                            sc.wait_ge(pe.sem, pe.at(n, f"TM{i}"))
                            if i == 0:
                                wait(sc, pool.sem, pool.at(n - 2, "vt"))
                            tm = bank(f"TM{i}")[:, 0:2 * TOKC].rearrange("p (t c) -> p t c", t=2)
                            nc.scalar.copy(vk[:, half, 2 * i:2 * i + 2, :], tm[:, :, 96:TOKC]).then_inc(act.sem, 1)
                groups(body)(sc)
                sc.wait_ge(dve.sem, dve.at(NG - 1, "g3"))
                g = GT[:].rearrange("p u t c -> p (u t c)")
                nc.scalar.activation(g, g, ACT.Exp, scale=-1.0).then_inc(s_gate, 1)

            @block.vector
            def _(ve):
                for t in range(TILES):
                    if t % 8 == 0:
                        ve.wait_ge(s_x[t // 8], 16)
                    nc.vector.bn_stats(out=stat[:, t, :], in_=X[:, t, :]).then_inc(s_ln, 1)
                for t in range(TILES):
                    ve.wait_ge(s_ln, t + 1)
                    nc.vector.bn_aggr(out=mv[:, t, :], in_=stat[:, t, :]).then_inc(s_ln, 1)
                ve.wait_ge(s_ln, 2 * TILES)
                nc.vector.tensor_scalar(var[:], mv[:, :, 1], EPS, None, ALU.add).then_inc(s_ln, 1)
                ve.wait_ge(s_sq, 1)
                nc.vector.reciprocal(rstd[:], rstd[:]).then_inc(s_ln, 1)
                for i, step in enumerate(NEWTON):
                    ve.wait_ge(s_ln, 2 * TILES + 2 + i)
                    newton(nc, step, rstd[:], var[:], scr[:]).then_inc(s_ln, 1)
                ve.wait_ge(s_w, 160)
                ve.wait_ge(s_ln, 2 * TILES + 2 + len(NEWTON))

                def normalise(n, half):
                    for j in range(4):
                        if j == 0:
                            wait(ve, pe.sem, pe.at(n - 2, "T1"))
                        t = 4 * n + j
                        nc.vector.tensor_scalar(xn[:, half, j, :], X[:, bass.ds(t, 1), :].rearrange("p a c -> p (a c)"),
                                                mv[:, bass.ds(t, 1), 0], rstd[:, bass.ds(t, 1)],
                                                ALU.subtract, ALU.mult).then_inc(s_xn, 1)

                def body(ve, b):
                    for half in range(2):
                        n = 2 * b + half
                        col = half * GRP
                        if not (isinstance(n, int) and n == NG - 1):
                            normalise(n + 1, 1 - half)
                        for f in range(2):
                            ve.wait_ge(act.sem, act.at(n, f"qh{f}"))
                            if f == 0:
                                wait(ve, pool.sem, pool.at(n - 2, "rkl"))
                            nc.vector.tensor_tensor(tcos[:, half, f, :], bank(f"Q{f}"),
                                                    rope_q[:, 0, col:col + GRP], ALU.mult).then_inc(dve.sem, 1)
                            nc.vector.tensor_tensor(qres[:, half, f, :], bank(f"Q{f}"),
                                                    split[:, half, f, 0, :], ALU.subtract).then_inc(dve.sem, 1)
                            ve.wait_ge(pe.sem, pe.at(n, f"S{f}"))
                            nc.vector.tensor_tensor(tsin[:, half, f, :], bank(f"S{f}"),
                                                    rope_q[:, 1, col:col + GRP], ALU.mult).then_inc(dve.sem, 1)
                            ve.wait_ge(act.sem, act.at(n, f"qm{f}"))
                            nc.vector.tensor_tensor(split[:, half, f, 2, :], qres[:, half, f, :],
                                                    split[:, half, f, 1, :], ALU.subtract).then_inc(dve.sem, 1)
                            kname, dst = (("K", kcos), ("KS", ksin))[f]
                            ve.wait_ge(pe.sem, pe.at(n, kname))
                            nc.vector.tensor_tensor(dst[:, half, :], bank(kname)[0:64],
                                                    rope_k[:, f, col:col + GRP], ALU.mult).then_inc(dve.sem, 1)
                        for j in range(4):
                            ve.wait_ge(act.sem, act.at(n, f"tm{j // 2}"))
                            z = bank(f"TM{j // 2}")[:, TOKC * (j % 2):TOKC * (j % 2) + 96]
                            nc.vector.tensor_tensor(GT[:, bass.ds(b * HA, HA), 4 * half + j, :],
                                                    z.rearrange("p (h c) -> p h c", h=HA),
                                                    bgate[:].rearrange("p (h c) -> p h c", h=HA),
                                                    ALU.add).then_inc(dve.sem, 1)
                normalise(0, 0)
                groups(body)(ve)
                g = GT[:].rearrange("p u t c -> p (u t c)")
                ve.wait_ge(s_gate, 1)
                nc.vector.tensor_scalar(g, g, 1.0, None, ALU.add).then_inc(s_gate, 1)
                ve.wait_ge(s_gate, 2)
                nc.vector.reciprocal(g, g).then_inc(s_gate, 1)

            @block.gpsimd
            def _(po):
                nc.gpsimd.memset(G["VS"][0:64], 0.0)

                def body(po, b):
                    for half in range(2):
                        n = 2 * b + half
                        for f in range(2):
                            po.wait_ge(dve.sem, dve.at(n, f"s{f}"))
                            nc.gpsimd.tensor_tensor(tcos[:, half, f, :], tcos[:, half, f, :], tsin[:, half, f, :],
                                                    ALU.add).then_inc(pool.sem, 1)
                            po.wait_ge(act.sem, act.at(n, f"rh{f}"))
                            nc.gpsimd.tensor_tensor(rres[:, half, f, :], tcos[:, half, f, :], split[:, half, f, 3, :],
                                                    ALU.subtract).then_inc(pool.sem, 1)
                            po.wait_ge(dve.sem, dve.at(n, f"l{f}"))
                            po.wait_ge(act.sem, act.at(n, f"rm{f}"))
                            nc.gpsimd.tensor_tensor(split[:, half, f, 5, :], rres[:, half, f, :],
                                                    split[:, half, f, 4, :], ALU.subtract).then_inc(pool.sem, 1)
                        po.wait_ge(dve.sem, dve.at(n, "sk"))
                        nc.gpsimd.tensor_tensor(kcos[:, half, :], kcos[:, half, :], ksin[:, half, :],
                                                ALU.add).then_inc(pool.sem, 1)
                        po.wait_ge(act.sem, act.at(n, "kh"))
                        nc.gpsimd.tensor_tensor(kres[:, half, :], kcos[:, half, :], ksplit[:, half, 0, :],
                                                ALU.subtract).then_inc(pool.sem, 1)
                        po.wait_ge(act.sem, act.at(n, "km"))
                        nc.gpsimd.tensor_tensor(ksplit[:, half, 2, :], kres[:, half, :], ksplit[:, half, 1, :],
                                                ALU.subtract).then_inc(pool.sem, 1)
                        po.wait_ge(act.sem, act.at(n, "tm1"))
                        nc.gpsimd.tensor_copy(
                            VT[:, bass.ds(b, 1), :, 4 * half:4 * half + 4, :].rearrange("p b h t d -> p (b h) t d"),
                            vk[:, half, :, 0:64].rearrange("p t (h d) -> p h t d", h=HA)).then_inc(pool.sem, 1)
                groups(body)(po)


def compress_a(nc, sems, G, I, S):
    COLS = HA * B * NBLK
    with ExitStack() as ctx:
        m = Mem(nc, ctx)
        kvr = m.sb("c_rows", [P, 2, BLK, P])
        kvh = m.sb("c_head_rows", [P, 2, 2 * HA, BLK, DA])
        w1 = m.sb("c_w1", [P, 2, P])
        w2 = m.sb("c_w2", [P, 2, DA])
        pos = m.sb("c_pos", [P, 2, HA])
        b1 = m.sb("c_b1", [P, 2])
        b2k = m.sb("c_b2k", [DA, 1])
        b2v = m.sb("c_b2v", [P, DA])
        memk = m.sb("c_memk", [DA, HA])
        xT = m.sb("c_xT", [P, 2, HA, 2, P])
        h1 = m.sb("c_h1", [P, 2, COLS])
        ck = m.sb("c_ck", [DA, HA, B, NBLK])
        ckres = m.sb("c_ckres", [DA, HA, B, NBLK])
        cks = m.sb("c_cks", [DA, 3, HA, B, NBLK], BF16)
        cv = m.sb("c_cv", [P, HA, 2, DA])
        psum = m.ps("c_psum")
        ident = G["ident"]
        s_w = sems("c_weights_loaded")
        s_g = sems("c_heads_gathered")
        s_t = sems("c_transposed")
        s_e = sems("c_evacuated")
        s_h = sems("c_hidden_ready")
        s_r = sems("c_relu_done")
        s_o = sems("c_second_layer")
        s_v = sems("c_vector_steps")
        s_d = sems("c_written")
        s_m = sems("c_memory_written")

        with nc.Block() as block:
            @block.sync
            def _(sp):
                for hf in range(2):
                    sp.dma_start(kvr[:, hf], S["vkd"][hf * 2 * N:(hf + 1) * 2 * N, :]
                                 .rearrange("(r t) c -> r t c", t=BLK)).then_inc(s_w, 16)
                for i, kind in enumerate(("k", "v")):
                    for dst, src in ((w1[:, i], I[f"{kind}_cw1"]), (w2[:, i], I[f"{kind}_cw2"]),
                                     (pos[:, i], I[f"{kind}_pos"]), (b1[:, i:i + 1], I[f"{kind}_cb1"])):
                        sp.dma_start(dst, src[:]).then_inc(s_w, 16)
                sp.dma_start(b2k[:], I["k_cb2"][:]).then_inc(s_w, 16)
                sp.dma_start(b2v[:], rows(I["v_cb2"], 0, [(0, P), (1, DA)])).then_inc(s_w, 16)
                sp.dma_start(memk[:], I["mem_ck"][:]).then_inc(s_w, 16)
                for b in range(B):
                    sp.dma_start(S["cvd"][b * HA:(b + 1) * HA, NBLK - 1, :], I["mem_cv"][:]).then_inc(s_m, 16)
                sp.wait_ge(s_v, 2 + 4 + 4)
                for s in range(3):
                    for b in range(B):
                        sp.dma_start(S["ckd"][s, :, b * HA:(b + 1) * HA, :], cks[:, s, :, b, :]).then_inc(s_d, 16)
                for b in range(B):
                    low = (b % 2) * NBLK
                    sp.dma_start(S["cvd"][b * HA:(b + 1) * HA, 0:NBLK - 1, :].rearrange("h n d -> n h d"),
                                 cv[low:low + NBLK - 1, :, b // 2, :]).then_inc(s_d, 16)
                sp.wait_ge(s_d, 16 * 16)
                sp.wait_ge(s_m, 4 * 16)

            @block.tensor
            def _(te):
                te.wait_ge(s_w, 13 * 16)
                te.wait_ge(s_g, 2)
                for n in range(8):
                    kind, hp = n // 4, n % 4
                    for j in range(4):
                        h, hf = 2 * hp + j // 2, j % 2
                        head = (HA if kind == 0 else 0) + h
                        last = nc.tensor.transpose(psum[:, n, P * j:P * j + P],
                                                   kvh[:, hf, head].rearrange("p t d -> p (t d)"), ident[:])
                    last.then_inc(s_t, 1)
                for n in range(8):
                    kind, c = n // 4, n % 4
                    te.wait_ge(s_e, n + 1)
                    nc.tensor.matmul(psum[:, n, :], w1[:, kind, :],
                                     xT[:, kind, 2 * c:2 * c + 2, :, :].rearrange("p h f r -> p (h f r)"),
                                     start=True, stop=True).then_inc(s_h, 1)
                for c in range(4):
                    te.wait_ge(s_r, c + 1)
                    nc.tensor.matmul(psum[0:DA, c, :], w2[:, 0, :], h1[:, 0, GRP * c:GRP * c + GRP],
                                     start=True, stop=True).then_inc(s_o, 1)
                te.wait_ge(s_r, 8)
                for c in range(HA * 2):
                    last = nc.tensor.matmul(psum[:, 4, DA * c:DA * c + DA], h1[:, 1, P * c:P * c + P], w2[:, 1, :],
                                            start=True, stop=True)
                last.then_inc(s_o, 1)

            @block.scalar
            def _(sc):
                sc.wait_ge(s_w, 13 * 16)
                nc.scalar.copy(kvh[:, 1], kvr[:, 1].rearrange("p t (h d) -> p h t d", d=DA)).then_inc(s_g, 1)
                for n in range(8):
                    kind, c = n // 4, n % 4
                    sc.wait_ge(s_h, n + 1)
                    nc.scalar.activation(h1[:, kind, GRP * c:GRP * c + GRP], psum[:, n, :], ACT.Relu,
                                         bias=b1[:, kind:kind + 1]).then_inc(s_r, 1)

            @block.vector
            def _(ve):
                ve.wait_ge(s_w, 13 * 16)
                nc.vector.tensor_copy(kvh[:, 0], kvr[:, 0].rearrange("p t (h d) -> p h t d", d=DA)).then_inc(s_g, 1)
                for n in range(8):
                    kind, hp = n // 4, n % 4
                    ve.wait_ge(s_t, n + 1)
                    for j in range(2):
                        h = 2 * hp + j
                        last = nc.vector.tensor_scalar(xT[:, kind, h, :, :].rearrange("p f r -> p (f r)"),
                                                       psum[:, n, 2 * P * j:2 * P * j + 2 * P],
                                                       pos[:, kind, h:h + 1], None, ALU.add)
                    last.then_inc(s_e, 1)
                for c in range(4):
                    ve.wait_ge(s_o, c + 1)
                    nc.vector.tensor_scalar(ck[:, 2 * c:2 * c + 2, :, :].rearrange("p h b n -> p (h b n)"),
                                            psum[0:DA, c, :], b2k[:], None, ALU.add).then_inc(s_v, 1)
                ve.wait_ge(s_v, 4)
                nc.vector.tensor_copy(ck[:, :, :, NBLK - 1],
                                      memk[:].unsqueeze(2).broadcast_to([DA, HA, B])).then_inc(s_v, 1)
                flat = "p h b n -> p (h b n)"
                ve.wait_ge(s_v, 5)
                nc.vector.tensor_copy(cks[:, 0].rearrange(flat), ck[:].rearrange(flat)).then_inc(s_v, 1)
                ve.wait_ge(s_v, 6)
                nc.vector.tensor_tensor(ckres[:].rearrange(flat), ck[:].rearrange(flat), cks[:, 0].rearrange(flat),
                                        ALU.subtract).then_inc(s_v, 1)
                ve.wait_ge(s_v, 7)
                nc.vector.tensor_copy(cks[:, 1].rearrange(flat), ckres[:].rearrange(flat)).then_inc(s_v, 1)
                ve.wait_ge(s_v, 8)
                nc.vector.tensor_tensor(cks[:, 2].rearrange(flat), ckres[:].rearrange(flat), cks[:, 1].rearrange(flat),
                                        ALU.subtract).then_inc(s_v, 1)
                ve.wait_ge(s_o, 5)
                nc.vector.tensor_tensor(cv[:].rearrange("p h f d -> p (h f) d"),
                                        psum[:, 4, 0:HA * 2 * DA].rearrange("p (c d) -> p c d", d=DA),
                                        b2v[:].unsqueeze(1).broadcast_to([P, HA * 2, DA]), ALU.add).then_inc(s_v, 1)


R_MAX, R_WMAX, R_BLK = 48, 50, 64
PAD = 64
VW = 32
VB = DA + 1

A_BANKS = [(T, kind, i) for T in range(4)
           for kind, i in [("c", 0), ("w", 2 * T), ("w", 2 * T + 1)]
           + [("f", 2 * kt + gp) for kt in range(2 * T + 1) for gp in range(2)] + [("h", 2 * T + 1)]]
NBANK = len(A_BANKS)
A_FINE = []
for _t in range(QT):
    _keys = P * (_t + 1)
    for _lo in range(0, _keys, GRP):
        _len = min(GRP, _keys - _lo)
        _ng = 2 if _keys == P else max(1, min(GA, GRP // _len))
        A_FINE += [(_t, _g, _ng, _lo, _len) for _g in range(0, GA, _ng)]
NRING = 4 + 1 + 2 * QT + len(A_FINE)


OUT_STEPS = ("rcp", "wgt", "prod", "sum")


def ring_plan(first, last):
    plan = []
    for k, T in ([] if first else [(5, 3)]) + [(11, 0), (21, 1), (35, 2)]:
        plan += [(k, "O", T)] + [(k + 1 + i, step, T) for i, step in enumerate(OUT_STEPS)]
    if not last:
        plan += [(4 + c // 2, "comp", c) for c in range(4)] + [(6, "imp", 0)]
        plan += [(8 + i // 2, "win", i) for i in range(2 * QT)]
        plan += [(20 + (j * 21) // len(A_FINE), "fine", j) for j in range(len(A_FINE))]
    return sorted(plan, key=lambda e: e[0])


UNIT0_PLAN = [e for e in ring_plan(False, False) if e[1] in ("comp", "imp", "win", "fine")]


A_CHAIN = {("imp", 0): ["mem", "imax"], ("win", 1): ["esum", "thr"],
           ("win", 2): ["gt"] + [f"top{i}" for i in range(4)], ("win", 3): [f"top{i}" for i in range(4, 8)],
           ("win", 4): [f"rep{i}" for i in range(4)], ("win", 5): [f"rep{i}" for i in range(4, 8)],
           ("win", 6): ["sel"], ("win", 7): ["own"], ("win", 8): ["bias"],
           ("win", 9): ["chi"], ("win", 10): ["clo"],
           ("fine", len(A_FINE) - 1): ["join", "hi", "lo"]}
A_STEPS = [s for key in sorted(A_CHAIN, key=lambda k: (["imp", "win", "fine"].index(k[0]), k[1])) for s in A_CHAIN[key]]


def attention_a(nc, sems, G, I, S):
    with ExitStack() as ctx:
        m = Mem(nc, ctx)
        Qf = [m.sb(f"Qf{p}", [P, GA, N], BF16) for p in range(2)]
        Qc = [m.sb(f"Qc{p}", [P, GA, N], BF16) for p in range(2)]
        Kf = [m.sb(f"Kf{p}", [P, PAD + N], BF16) for p in range(2)]
        Kw = [m.sb(f"Kw{p}", [P, PAD + N], BF16) for p in range(2)]
        Kc = [m.sb(f"Kc{p}", [P, NBLK], BF16) for p in range(2)]
        Vf = [m.sb(f"Vf{p}", [P, QT, VW]) for p in range(2)]
        Va = [m.sb(f"Va{p}", [P, QT, VW]) for p in range(2)]
        Vs = [m.sb(f"Vs{p}", [P, QT, VW]) for p in range(2)]
        Vc = [m.sb(f"Vc{p}", [P, VW]) for p in range(2)]
        NP = 6
        probs = m.sb("A_probs", [P, NP, GRP])
        identb = m.sb("A_identb", [P, P], BF16)
        caus_q = m.sb("A_causal_q", [P, P], BF16)
        caus_k = m.sb("A_causal_k", [P, P], BF16)
        band_q = m.sb("A_band_q", [P, 2, 192], BF16)
        band_k = m.sb("A_band_k", [P, 2, WIN], BF16)
        own = m.sb("A_own", [P, QT, NBLK])
        mx = m.sb("A_max", [P, 3, GA, QT])
        mx2 = m.sb("A_max2", [P, GA, QT])
        mxs = m.sb("A_maxsplit", [P, 2, 3 * GA * QT], BF16)
        imax = m.sb("A_impmax", [P, QT])
        esum = m.sb("A_expsum", [P, QT])
        imp = m.sb("A_imp", [P, QT, NBLK])
        gt = m.sb("A_above", [P, QT, NBLK])
        top = m.sb("A_top", [P, QT, NSEL])
        rep = m.sb("A_rep", [P, QT, NBLK])
        selb = m.sb("A_selected", [P, QT, NBLK])
        bias = m.sb("A_bias", [P, QT, NBLK], BF16)
        biasT = m.sb("A_biasT", [NBLK, N], BF16)
        mT1 = m.sb("A_maxT_comp", [GA * QT, 2, P], BF16)
        mT2 = m.sb("A_maxT", [2 * GA * QT, 2, P], BF16)
        osb = m.sb("A_out_cols", [P, 2, 2 * P])
        och = m.sb("A_out_rows", [P, 2, 2 * GA, 3, VB])
        orc = m.sb("A_weights", [P, 2, 2 * GA, 3])
        opr = m.sb("A_products", [P, 2, 2 * GA, 3, DA])
        att = [m.sb(f"A_att{p}", [P, QT, GA * DA]) for p in range(2)]
        psum = m.ps("A_psum")
        GT = G["GT"][:].rearrange("p u t c -> p u (t c)")
        VT = G["VT"][:].rearrange("p b h t d -> p (b h) t d")
        VS = G["VS"][:].rearrange("p b h t d -> p (b h) t d")
        ident = G["ident"]
        turned = psum[:, 7, :].bitcast(BF16)

        s_c = sems("a_constants_loaded")
        s_ones = sems("a_value_operands_cleared")
        s_ld = [sems(f"a_unit_loaded{p}") for p in range(2)]
        s_lc = [sems(f"a_comp_operands_loaded{p}") for p in range(2)]
        s_v = sems("a_values_filled")
        s_st = sems("a_scores_ready")
        s_p = sems("a_probs_ready")
        s_pv = sems("a_probs_used")
        s_r = sems("a_ring_filled")
        s_rf = sems("a_ring_read")
        s_x = sems("a_turned_ready")
        s_xf = sems("a_turned_read")
        s_e = sems("a_block_exp_done")
        s_oc = sems("a_out_cols_ready")
        s_b = sems("a_bias_rows_loaded")
        s_m1 = sems("a_comp_max_rows_loaded")
        s_m2 = sems("a_max_rows_loaded")
        s_aw = [sems(f"a_out_written{p}") for p in range(2)]
        chain = Steps(sems("a_selection_steps"), A_STEPS)
        outs = Steps(sems("a_output_steps"), [f"{s}{T}" for T in range(4) for s in OUT_STEPS])
        LOADS_C, LOADS = 7 * 16, 12 * 16

        def program(block_body, unit0, tail):
            def run(eng):
                unit0(eng)
                block_body(eng, 0, 0, 0, True, False)
                with eng.Fori(0, (UA - 2) // 2) as i:
                    for p in (1, 0):
                        block_body(eng, 2 * i + (2 - p), i + (1 - p), p, False, False)
                block_body(eng, UA - 1, UA // 2 - 1, 1, False, True)
                tail(eng)
            return run


        def ring_base(u, first):
            return NRING - 1 + (NRING + 4) * u + int(first)

        def ring_read(u, last, tag, i):
            ring = [e[1:] for e in ring_plan(False, last) if e[1] not in OUT_STEPS]
            return ring_base(u, False) + ring.index((tag, i)) + 1

        RING = 3

        with nc.Block() as block:
            @block.sync
            def _(sp):
                bf = lambda name: I[name].bitcast(BF16)
                for dst, src in ((identb, bf("identb")), (caus_q, bf("causal_q")), (caus_k, bf("causal_k")),
                                 (band_q, bf("band_q")), (band_k, bf("band_k")), (own, I["own"])):
                    sp.dma_start(dst[:], src).then_inc(s_c, 16)
                for p in range(2):
                    for buf, name in ((Qc, "qc_rows"), (Kf, "kf_rows"), (Kw, "kw_rows"), (Kc, "kc_rows")):
                        sp.dma_start(buf[p][R_MAX:P], bf(name)).then_inc(s_c, 16)
                    sp.dma_start(Qf[p][R_MAX:P], bf("zero_rows")).then_inc(s_aw[p], 16)

                def load(u, p):
                    un = bass.ds(u, 1)
                    qd = S["qd"].rearrange("s b (h d g) t -> s (b h) d (g t)", h=HA, g=GA)
                    kd = S["kd"].rearrange("s b (h d) t -> s (b h) d t", h=HA)
                    def query(Q, first, sem):
                        row = 0
                        for n in (3, 2, 1):
                            sp.dma_start(Q[p][row:row + DA * n].rearrange("r g t -> r (g t)"),
                                         qd[first:first + n, un].rearrange("s u d x -> (s u) d x")).then_inc(sem[p], 16)
                            row += DA * n

                    def key(dst, src, sem):
                        row = 0
                        for part, reps in enumerate((3, 2, 1)):
                            sp.dma_start(dst[row:row + DA * reps], src(part, reps)).then_inc(sem[p], 16)
                            row += DA * reps
                    query(Qc, 0, s_lc)
                    sp.dma_start(Qc[p][R_MAX:R_MAX + 2], bf("zero_rows")[0:2]).then_inc(s_lc[p], 16)
                    key(Kc[p][:, :], lambda part, reps: S["ckd"][part, :, un, :].rearrange("d u n -> u d n")
                        .broadcast_to([reps, DA, NBLK]), s_lc)
                    query(Qf, 3, s_ld)
                    sp.dma_start(Qf[p][R_MAX:R_MAX + 4], bf("zero_rows")[0:4]).then_inc(s_ld[p], 16)
                    for K in (Kw, Kf):
                        key(K[p][:, PAD:PAD + N], lambda part, reps: kd[part, un].broadcast_to([reps, DA, N]), s_ld)
                    for low in (0, NBLK):
                        sp.dma_start(Vc[p][low:low + NBLK, 0:DA],
                                     S["cvd"][un].rearrange("u n d -> (u n) d")).then_inc(s_ld[p], 16)

                def first_half(u, p):
                    sp.wait_ge(s_xf, 3 * u + 1)
                    sp.dma_start(Qf[p][R_BLK:P], biasT[:].unsqueeze(1).broadcast_to([NBLK, GA, N])).then_inc(s_b, 16)
                    sp.wait_ge(s_xf, 3 * u + 2)
                    for s in range(2):
                        sp.dma_start(Qc[p][R_MAX + s:R_MAX + s + 1].rearrange("r g (t q) -> r (g t) q", q=P),
                                     mT1[:, s, :]).then_inc(s_m1, 16)

                def second_max(u, p):
                    sp.wait_ge(s_xf, 3 * u + 3)
                    for i, row in enumerate((R_WMAX, R_MAX)):
                        for s in range(2):
                            sp.dma_start(Qf[p][row + s:row + s + 1].rearrange("r g (t q) -> r (g t) q", q=P),
                                         mT2[GA * QT * i:GA * QT * (i + 1), s, :]).then_inc(s_m2, 16)

                def store(u, p):
                    sp.wait_ge(outs.sem, outs.at(u, "sum3"))
                    sp.dma_start(S["att"][bass.ds(u, 1)].rearrange("u p c -> (u p) c"),
                                 att[p][:].rearrange("p t c -> p (t c)")).then_inc(s_aw[p], 16)

                def unit0(sp):
                    sp.wait_ge(s_ones, 16)
                    load(0, 0)
                    first_half(0, 0)
                    second_max(0, 0)

                def body(sp, u, r, p, first, last):
                    if not last:
                        wait(sp, s_pv, NBANK * u)
                        load(u + 1, 1 - p)
                    if not first:
                        store(u - 1, 1 - p)
                    if not last:
                        first_half(u + 1, 1 - p)
                        second_max(u + 1, 1 - p)

                def tail(sp):
                    store(UA - 1, 1)
                    for p in range(2):
                        sp.wait_ge(s_aw[p], 16 * (UA // 2 + 1))
                program(body, unit0, tail)(sp)

            @block.tensor
            def _(te):
                def ring_slot(idx, place):
                    if place == 0:
                        wait(te, s_rf, idx)
                    elif place >= RING:
                        wait(te, s_rf, idx - RING + 1)
                    return psum[:, place % RING, :]

                def comp_max(p, c, out):
                    for t in range(2):
                        for g in range(GA):
                            row = P * (2 * c + t)
                            last = nc.tensor.matmul(out[:, (GA * t + g) * NBLK:(GA * t + g + 1) * NBLK],
                                                    Qc[p][:, g, row:row + P], Kc[p][:],
                                                    start=(t == 0 and g == 0), stop=True, skip_group_check=True)
                    last.then_inc(s_r, 1)

                def importance(p, out):
                    for t in range(QT):
                        for g in range(GA):
                            last = nc.tensor.matmul(out[:, NBLK * t:NBLK * t + NBLK], Qc[p][:, g, P * t:P * t + P],
                                                    Kc[p][:], start=(t == 0 and g == 0), stop=(g == GA - 1),
                                                    skip_group_check=True)
                    last.then_inc(s_r, 1)

                def window_max(p, i, out):
                    t, g0 = i // 2, 2 * (i % 2)
                    o = out[:, 0:2 * 192].rearrange("p (g k) -> p g k", g=2)
                    nc.tensor.matmul(o, identb[:], band_q[:, min(t, 1):min(t, 1) + 1, :].broadcast_to([P, 2, 192]),
                                     start=True, stop=True, skip_group_check=True)
                    for g in range(2):
                        last = nc.tensor.matmul(o[:, g, :], Qf[p][:, g0 + g, P * t:P * t + P],
                                                Kw[p][:, P * t:P * t + 192], start=False, stop=True, skip_group_check=True)
                    last.then_inc(s_r, 1)

                def fine_max(p, j, out):
                    t, g0, ng, lo, n = A_FINE[j]
                    o = out[:, 0:ng * n].rearrange("p (g k) -> p g k", g=ng)
                    diag = lo <= P * t < lo + n
                    for g in range(ng):
                        last = nc.tensor.matmul(o[:, g, :], Qf[p][:, g0 + g, P * t:P * t + P],
                                                Kf[p][:, PAD + lo:PAD + lo + n], start=(g == 0), stop=True,
                                                skip_group_check=True)
                    if diag:
                        last = nc.tensor.matmul(o[:, :, P * t - lo:P * t - lo + P], identb[:],
                                                caus_q[:].unsqueeze(1).broadcast_to([P, ng, P]), start=False, stop=True,
                                                skip_group_check=True)
                    last.then_inc(s_r, 1)

                def turn_bias(u):
                    for t in range(QT):
                        last = nc.tensor.transpose(turned[0:NBLK, P * t:P * t + P], bias[:, t, :], identb[:])
                    last.then_inc(s_x, 1)

                def turn_max(u, which):
                    lo, n, step = ((0, GA * QT, "clo"), (GA * QT, 2 * GA * QT, "lo"))[which]
                    if which == 0 or isinstance(u, int):
                        te.wait_ge(chain.sem, chain.at(u, step))
                        te.wait_ge(s_xf, 3 * u + 1 + which)
                    for s in range(2):
                        last = nc.tensor.transpose(turned[0:n, P * s:P * s + P], mxs[:, s, lo:lo + n], identb[:])
                    last.then_inc(s_x, 1)

                def slot(u1, r1, p1, tag, i, out):
                    if tag == "comp":
                        if i == 0:
                            te.wait_ge(s_lc[p1], LOADS_C * (r1 + 1))
                        comp_max(p1, i, out)
                    elif tag == "imp":
                        importance(p1, out)
                    elif tag == "win":
                        if i == 0:
                            te.wait_ge(s_ld[p1], LOADS * (r1 + 1))
                        window_max(p1, i, out)
                    else:
                        if i == 0:
                            te.wait_ge(s_b, 16 * (u1 + 1))
                        fine_max(p1, i, out)

                def scores(u, p, k):
                    T, kind, i = A_BANKS[k]
                    n = NBANK * u + k
                    wait(te, s_p, n - 1)
                    out = psum[:, 3 + k % 2, :]
                    q = Qf[p]
                    if kind == "c":
                        for hp in range(2):
                            last = nc.tensor.matmul(out[64 * hp:64 * hp + 64], Kc[p][:],
                                                    Qc[p][:, 2 * hp:2 * hp + 2, 2 * P * T:2 * P * (T + 1)],
                                                    start=True, stop=True)
                    elif kind == "w":
                        o = out.rearrange("p (w g q) -> p w g q", w=2, g=GA)
                        if i == 0:
                            for w in range(2):
                                nc.tensor.matmul(o[:, w], identb[:], band_k[:, w:w + 1, :].broadcast_to([P, GA, WIN]),
                                                 start=(w == 0), stop=True, skip_group_check=True)
                        else:
                            nc.tensor.matmul(out.rearrange("p (x q) -> p x q", q=WIN), identb[:],
                                             band_k[:, 1:2, :].broadcast_to([P, 2 * GA, WIN]), start=True, stop=True,
                                             skip_group_check=True)
                        for w in range(2):
                            lo = WIN * (2 * i + w)
                            last = nc.tensor.matmul(o[:, w], Kw[p][:, lo:lo + P], q[:, :, lo:lo + WIN],
                                                    start=False, stop=True, skip_group_check=True)
                    elif kind == "f":
                        kt, gp = i // 2, i % 2
                        diag = kt == 2 * T
                        last = nc.tensor.matmul(out, Kf[p][:, PAD + P * kt:PAD + P * kt + P],
                                                q[:, 2 * gp:2 * gp + 2, 2 * P * T:2 * P * (T + 1)],
                                                start=True, stop=True, skip_group_check=True)
                        if diag:
                            o = out.rearrange("p (g q) -> p g q", g=2)[:, :, 0:P]
                            last = nc.tensor.matmul(o, identb[:], caus_k[:].unsqueeze(1).broadcast_to([P, 2, P]),
                                                    start=False, stop=True, skip_group_check=True)
                    else:
                        nc.tensor.matmul(out, Kf[p][:, PAD + P * i:PAD + P * i + P],
                                         q[:, :, P * i:P * i + P], start=True, stop=True, skip_group_check=True)
                        last = nc.tensor.matmul(out.rearrange("p (g q) -> p g q", g=GA), identb[:],
                                                caus_k[:].unsqueeze(1).broadcast_to([P, GA, P]), start=False, stop=True, skip_group_check=True)
                    last.then_inc(s_st, 1)

                def values(u, p, k):
                    T, kind, i = A_BANKS[k]
                    if kind != "c":
                        te.wait_ge(s_p, NBANK * u + k + 1)
                    acc = psum[:, 5 + T % 2, :]
                    pr = probs[:, k % NP, :]
                    for w in range(2 if kind == "w" else 1):
                        for g in range(GA):
                            o = acc[32 * g:32 * g + 32]
                            if kind == "c":
                                h = 64 * (g // 2)
                                last = nc.tensor.matmul(o[:, 0:2 * P], Vc[p][h:h + 64, :],
                                                        pr[h:h + 64, 2 * P * (g % 2):2 * P * (g % 2 + 1)],
                                                        start=True, stop=True, skip_group_check=True)
                            elif kind == "w":
                                col = P * (i % 2) + WIN * w
                                last = nc.tensor.matmul(o[:, col:col + WIN], (Vs, Va)[w][p][:, i, :],
                                                        pr[:, WIN * (GA * w + g):WIN * (GA * w + g + 1)],
                                                        start=False, stop=True, skip_group_check=True)
                            elif kind == "f":
                                pr2 = probs[:, (k - 1 + g // 2) % NP, 2 * P * (g % 2):2 * P * (g % 2 + 1)]
                                last = nc.tensor.matmul(o[:, 0:2 * P], Vf[p][:, i // 2, :], pr2,
                                                        start=False, stop=True, skip_group_check=True)
                            else:
                                last = nc.tensor.matmul(o[:, P:2 * P], Vf[p][:, i, :], pr[:, P * g:P * g + P],
                                                        start=False, stop=True, skip_group_check=True)
                    last.then_inc(s_pv, 2 if kind == "f" else 1)

                def turn_output(u, T, out):
                    te.wait_ge(s_oc, 4 * u + T + 1)
                    for j in range(2):
                        last = nc.tensor.transpose(out[:, P * j:P * j + P], osb[:, T % 2, P * j:P * j + P], ident[:])
                    last.then_inc(s_r, 1)

                def unit0(te):
                    te.wait_ge(s_c, 16 * 14)
                    for p in range(2):
                        te.wait_ge(s_aw[p], 16)
                    for j, (_, tag, i) in enumerate(UNIT0_PLAN):
                        if (tag, i) == ("fine", 0):
                            te.wait_ge(chain.sem, chain.at(0, "bias"))
                            turn_bias(0)
                            turn_max(0, 0)
                        slot(0, 0, 0, tag, i, ring_slot(j, j))
                    turn_max(0, 1)

                def body(te, u, r, p, first, last):
                    plan = [e for e in ring_plan(first, last) if e[1] not in OUT_STEPS]
                    idx, place = ring_base(u, first), 0
                    te.wait_ge(s_m1, 32 * (u + 1))
                    te.wait_ge(s_v, u + 1)
                    for k in range(NBANK):
                        if k >= 2 and A_BANKS[k - 2][1] == "c":
                            te.wait_ge(s_p, NBANK * u + k - 1)
                            wait(te, s_oc, 4 * u + A_BANKS[k - 2][0] - 1)
                        if k == 15 and not last:
                            te.wait_ge(chain.sem, chain.at(u + 1, "bias"))
                            wait(te, s_xf, 3 * (u + 1))
                        if k == 43 and not last:
                            te.wait_ge(chain.sem, chain.at(u + 1, "lo"))
                            te.wait_ge(s_xf, 3 * (u + 1) + 2)
                        if k == 1:
                            te.wait_ge(s_m2, 64 * (u + 1))
                        scores(u, p, k)
                        if k >= 2 and not (A_BANKS[k - 2][1] == "f" and A_BANKS[k - 2][2] % 2 == 0):
                            values(u, p, k - 2)
                        if k == 15 and not last:
                            turn_bias(u + 1)
                        if k == 17 and not last:
                            turn_max(u + 1, 0)
                        for _, tag, i in [e for e in plan if e[0] == k]:
                            out = ring_slot(idx, place)
                            if tag == "O":
                                turn_output(u - 1 if i == 3 else u, i, out)
                            else:
                                slot(u + 1, r + p, 1 - p, tag, i, out)
                            idx, place = idx + 1, place + 1
                        if k == 43 and not last:
                            turn_max(u + 1, 1)
                    values(u, p, NBANK - 2)
                    values(u, p, NBANK - 1)

                def tail(te):
                    idx = ring_base(UA - 1, False) + 4
                    turn_output(UA - 1, 3, ring_slot(idx, 0))
                program(body, unit0, tail)(te)

            @block.scalar
            def _(sc):
                def exp_bank(u, k):
                    n = NBANK * u + k
                    sc.wait_ge(s_st, n + 1)
                    wait(sc, s_pv, n - NP + 1)
                    nc.scalar.activation(probs[:, k % NP, :], psum[:, 3 + k % 2, :], ACT.Exp,
                                         scale=SCALE_A).then_inc(s_p, 1)

                def block_exp(read):
                    sc.wait_ge(s_rf, read)
                    nc.scalar.activation(imp[:], imp[:], ACT.Exp, scale=SCALE_A / GA).then_inc(s_e, 1)

                def take_bias(u):
                    sc.wait_ge(s_x, 3 * u + 1)
                    wait(sc, s_b, 16 * u)
                    nc.scalar.copy(biasT[:], turned[0:NBLK, :]).then_inc(s_xf, 1)

                def take_max(u, which):
                    dst, n, by, each = ((mT1, GA * QT, s_m1, 32), (mT2, 2 * GA * QT, s_m2, 64))[which]
                    sc.wait_ge(s_x, 3 * u + 2 + which)
                    wait(sc, by, each * u)
                    nc.scalar.copy(dst[:].rearrange("p s q -> p (s q)"), turned[0:n, 0:2 * P]).then_inc(s_xf, 1)

                def take_output(u, T, u_last):
                    last = max(k for k, b in enumerate(A_BANKS) if b[0] == T)
                    sc.wait_ge(s_pv, NBANK * u + last + 1)
                    if T < 2:
                        if not (isinstance(u, int) and u == 0):
                            sc.wait_ge(s_rf, ring_read(u - 1, False, "O", 2) if T == 0 else ring_read(u, u_last, "O", 3))
                    else:
                        sc.wait_ge(s_rf, ring_read(u, u_last, "O", T - 2))
                    nc.scalar.copy(osb[:, T % 2, :], psum[:, 5 + T % 2, 0:2 * P]).then_inc(s_oc, 1)

                def unit0(sc):
                    block_exp(5)
                    take_bias(0)
                    take_max(0, 0)
                    take_max(0, 1)

                def body(sc, u, r, p, first, last):
                    for k in range(NBANK):
                        exp_bank(u, k)
                        if k == 3 and not first:
                            take_output(u - 1, 3, False)
                        if k in (9, 19, 33):
                            take_output(u, (9, 19, 33).index(k), last)
                        if last:
                            continue
                        if k == 8:
                            block_exp(ring_read(u, last, "imp", 0))
                        if k == 16:
                            take_bias(u + 1)
                        if k == 18:
                            take_max(u + 1, 0)
                        if k == 44:
                            take_max(u + 1, 1)

                def tail(sc):
                    take_output(UA - 1, 3, True)
                program(body, unit0, tail)(sc)

            @block.vector
            def _(ve):
                ve.wait_ge(s_c, 16 * 14)
                nc.vector.memset(selb[:], 0.0)
                nc.vector.memset(mx2[:], NEG)
                for p in range(2):
                    nc.vector.memset(Kf[p][0:R_MAX, 0:PAD], 0.0)
                    nc.vector.memset(Kw[p][0:R_MAX, 0:PAD], 0.0)
                operands = [(V[p], br) for p in range(2) for V, br in ((Vc, 0), (Vf, 1), (Va, 2), (Vs, 2))]
                for V, _ in operands:
                    nc.vector.memset(V[:], 0.0).then_inc(s_ones, 1)
                ve.wait_ge(s_ones, len(operands))
                for V, br in operands:
                    nc.vector.memset(V[..., VB * br + DA:VB * br + DA + 1], 1.0).then_inc(s_ones, 1)

                def maxima(u, tag, i, src):
                    if tag == "win" and i in (4, 5):
                        ve.wait_ge(chain.sem, chain.at(u, f"top{4 * (i - 4) + 3}"))
                    if tag == "comp":
                        nc.vector.reduce_max(mx[:, 0, :, 2 * i:2 * i + 2].rearrange("p g t -> p t g"),
                                             src.rearrange("p (t g n) -> p t g n", t=2, g=GA), AX).then_inc(s_rf, 1)
                    elif tag == "win":
                        t, g0 = i // 2, 2 * (i % 2)
                        nc.vector.reduce_max(mx[:, 1, g0:g0 + 2, t],
                                             src[:, 0:384].rearrange("p (g k) -> p g k", g=2), AX).then_inc(s_rf, 1)
                    elif tag == "fine":
                        t, g0, ng, lo, n = A_FINE[i]
                        dst = (mx2[:, g0:g0 + ng, t] if lo else mx[:, 2, g0:g0 + ng, t])
                        nc.vector.reduce_max(dst, src[:, 0:ng * n].rearrange("p (g k) -> p g k", g=ng), AX).then_inc(s_rf, 1)

                def selection(u, step, idx, src):
                    def after(name):
                        ve.wait_ge(chain.sem, chain.at(u, name))
                    nb = NBLK - 1
                    if step == "mem":
                        op = nc.vector.memset(src.rearrange("p (t n) -> p t n", t=QT)[:, :, nb], -1000.0 * GA / SCALE_A)
                    elif step == "imax":
                        after("mem")
                        op = nc.vector.reduce_max(imax[:], src.rearrange("p (t n) -> p t n", t=QT), AX)
                    elif step == "esum":
                        ve.wait_ge(s_e, u + 1)
                        op = nc.vector.reduce_sum(esum[:], imp[:], AX)
                    elif step == "thr":
                        after("esum")
                        op = nc.vector.tensor_scalar(esum[:], esum[:], 1e-10, None, ALU.mult)
                    elif step == "gt":
                        after("thr")
                        op = nc.vector.tensor_tensor(gt[:], imp[:], esum[:].unsqueeze(2).broadcast_to([P, QT, NBLK]), ALU.is_gt)
                    elif step.startswith("top"):
                        t = int(step[3:])
                        op = nc.vector.max(out=top[:, t, :], in_=imp[:, t, 0:nb])
                    elif step.startswith("rep"):
                        t = int(step[3:])
                        op = nc.vector.match_replace(out=rep[:, t, 0:nb], in_to_replace=top[:, t, :],
                                                     in_values=imp[:, t, 0:nb], imm_value=-1.0)
                    elif step == "sel":
                        after("rep7")
                        op = nc.vector.scalar_tensor_tensor(out=selb[:, :, 0:nb], in0=rep[:, :, 0:nb], scalar=0.0,
                                                            in1=gt[:, :, 0:nb], op0=ALU.is_lt, op1=ALU.mult)
                    elif step == "own":
                        after("sel")
                        op = nc.vector.tensor_tensor(rep[:], selb[:], own[:], ALU.max)
                    elif step == "bias":
                        after("own")
                        wait(ve, s_x, 3 * u)
                        op = nc.vector.tensor_scalar(bias[:], rep[:], -1.0, -NEG, ALU.add, ALU.mult)
                    elif step in ("chi", "clo", "hi", "lo"):
                        lo, n = (0, GA * QT) if step[0] == "c" else (GA * QT, 2 * GA * QT)
                        src = mx[:].rearrange("p b g t -> p (b g t)")[:, lo:lo + n]
                        hi = mxs[:, 0, lo:lo + n]
                        if step == "chi":
                            wait(ve, s_x, 3 * u)
                        if step[-2:] == "hi":
                            if step == "hi":
                                after("join")
                            else:
                                ve.wait_ge(s_rf, idx)
                            op = nc.vector.tensor_scalar(hi, src, -1.0, None, ALU.mult)
                        else:
                            after("chi" if step == "clo" else "hi")
                            op = nc.vector.scalar_tensor_tensor(out=mxs[:, 1, lo:lo + n], in0=src, scalar=-1.0,
                                                                in1=hi, op0=ALU.mult, op1=ALU.subtract)
                    else:
                        ve.wait_ge(s_rf, idx)
                        op = nc.vector.tensor_tensor(mx[:, 2], mx[:, 2], mx2[:], ALU.max)
                    op.then_inc(chain.sem, 1)

                def block_scores(u, src):
                    ve.wait_ge(chain.sem, chain.at(u, "imax"))
                    nc.vector.tensor_tensor(imp[:], src.rearrange("p (t n) -> p t n", t=QT),
                                            imax[:].unsqueeze(2).broadcast_to([P, QT, NBLK]),
                                            ALU.subtract).then_inc(s_rf, 1)

                def take(T, src):
                    nc.vector.tensor_copy(och[:, T % 2], src[:, 0:2 * P].rearrange("p (x r) -> p x r", r=32)[:, :, 0:3 * VB]
                                          .rearrange("p x (b c) -> p x b c", b=3)).then_inc(s_rf, 1)

                def output(u, r, p, T, step, taken):
                    z = T % 2
                    def after(name):
                        ve.wait_ge(outs.sem, outs.at(u, f"{name}{T}"))
                    if step == "rcp":
                        ve.wait_ge(s_rf, taken)
                        op = nc.vector.reciprocal(orc[:, z], och[:, z, :, :, DA])
                    elif step == "wgt":
                        after("rcp")
                        gate = GT[:, bass.ds(u, 1), 24 * T:24 * T + 24].rearrange("p u (x b) -> p (u x) b", b=3)
                        op = nc.vector.tensor_tensor(orc[:, z], orc[:, z], gate, ALU.mult)
                    elif step == "prod":
                        after("wgt")
                        op = nc.vector.tensor_tensor(opr[:, z], och[:, z, :, :, 0:DA],
                                                     orc[:, z].unsqueeze(3).broadcast_to([P, 2 * GA, 3, DA]), ALU.mult)
                    else:
                        after("prod")
                        if T == 0:
                            ve.wait_ge(s_aw[p], 16 * (r + 1))
                        op = nc.vector.reduce_sum(att[p][:, 2 * T:2 * T + 2, :].rearrange("p t (g d) -> p (t g) d", g=GA),
                                                  opr[:, z].rearrange("p x b d -> p x d b"), AX)
                    op.then_inc(outs.sem, 1)

                def unit0(ve):
                    for j, (_, tag, i) in enumerate(UNIT0_PLAN):
                        ve.wait_ge(s_r, j + 1)
                        src = psum[:, j % RING, :]
                        maxima(0, tag, i, src)
                        for step in A_CHAIN.get((tag, i), ()):
                            selection(0, step, j + 1, src)
                        if tag == "imp":
                            block_scores(0, src)

                def body(ve, u, r, p, first, last):
                    idx, place = ring_base(u, first), 0
                    for _, tag, i in ring_plan(first, last):
                        if tag in OUT_STEPS or tag == "O":
                            out_u, out_r, out_p = (u - 1, r - 1 + p, 1 - p) if i == 3 else (u, r, p)
                        if tag in OUT_STEPS:
                            output(out_u, out_r, out_p, i, tag, taken)
                            continue
                        ve.wait_ge(s_r, idx + 1)
                        src = psum[:, place % RING, :]
                        if tag == "O":
                            take(i, src)
                            taken = idx + 1
                        else:
                            maxima(u + 1, tag, i, src)
                            for step in A_CHAIN.get((tag, i), ()):
                                selection(u + 1, step, idx + 1, src)
                            if tag == "imp":
                                block_scores(u + 1, src)
                        idx, place = idx + 1, place + 1

                def tail(ve):
                    idx = ring_base(UA - 1, False) + 4
                    ve.wait_ge(s_r, idx + 1)
                    take(3, psum[:, 0, :])
                    for step in OUT_STEPS:
                        output(UA - 1, UA // 2 - 1, 1, 3, step, idx + 1)
                program(body, unit0, tail)(ve)

            @block.gpsimd
            def _(po):
                po.wait_ge(s_ones, 16)

                def fill(u, p):
                    un = bass.ds(u, 1)
                    for V, src, col in ((Vf, VT, VB), (Va, VT, 2 * VB), (Vs, VS, 2 * VB)):
                        op = nc.gpsimd.tensor_copy(V[p][:, :, col:col + DA], src[:, un].rearrange("p u t d -> p (u t) d"))
                    op.then_inc(s_v, 1)

                def unit0(po):
                    fill(0, 0)

                def body(po, u, r, p, first, last):
                    if not last:
                        wait(po, s_pv, NBANK * u)
                        fill(u + 1, 1 - p)
                program(body, unit0, lambda po: None)(po)


FC = HID // P


def ternarize(nc, sems, G, I):
    with ExitStack() as ctx:
        m = Mem(nc, ctx)
        mags = [m.sb(f"t_abs{i}", [P, FC * D]) for i in range(2)]
        negs = [m.sb(f"t_neg{i}", [P, FC * D]) for i in range(2)]
        ones = m.sb("t_ones", [P, P])
        sums = m.sb("t_sums", [P, 2])
        mean = m.sb("t_mean", [P, 2])
        thr = m.sb("t_thr", [P, 2])
        nthr = m.sb("t_nthr", [P, 2])
        psum = m.ps("t_psum")
        raw = [m.sb(f"t_raw{i}", [P, FC * D]) for i in range(2)]
        s_w, s_v, s_m = sems("t_loaded"), sems("t_steps"), sems("t_total")
        done = [G["wfc"][:].rearrange("p k h -> p (k h)"), G["wproj"][:].rearrange("p k d -> p (k d)")]

        with nc.Block() as block:
            @block.sync
            def _(sp):
                sp.dma_start(raw[0][:].rearrange("p (k h) -> p k h", k=2),
                             I["w_fc"].rearrange("(k p) h -> p k h", p=P)).then_inc(s_w, 16)
                sp.dma_start(raw[1][:].rearrange("p (k d) -> p k d", k=FC),
                             I["w_proj"].rearrange("(k p) d -> p k d", p=P)).then_inc(s_w, 16)

            @block.tensor
            def _(te):
                te.wait_ge(s_v, 5)
                nc.tensor.matmul(psum[:, 0, 0:2], ones[:], sums[:], start=True, stop=True).then_inc(s_m, 1)

            @block.vector
            def _(ve):
                def step(n, op):
                    op.then_inc(s_v, 1)
                    ve.wait_ge(s_v, n)
                nc.vector.memset(ones[:], 1.0).then_inc(s_v, 1)
                ve.wait_ge(s_w, 32)
                for i in range(2):
                    nc.vector.scalar_tensor_tensor(out=mags[i][:], in0=raw[i][:], scalar=-1.0, in1=raw[i][:],
                                                   op0=ALU.mult, op1=ALU.max).then_inc(s_v, 1)
                ve.wait_ge(s_v, 3)
                for i in range(2):
                    nc.vector.reduce_sum(sums[:, i:i + 1], mags[i][:], AX).then_inc(s_v, 1)
                ve.wait_ge(s_m, 1)
                step(6, nc.vector.tensor_scalar(mean[:], psum[:, 0, 0:2], 1.0 / (D * HID), 1e-5, ALU.mult, ALU.max))
                step(7, nc.vector.tensor_scalar(thr[:], mean[:], 0.7, None, ALU.mult))
                step(8, nc.vector.tensor_scalar(nthr[:], thr[:], -1.0, None, ALU.mult))
                for i in range(2):
                    nc.vector.tensor_scalar(mags[i][:], raw[i][:], thr[:, i:i + 1], mean[:, i:i + 1],
                                            ALU.is_gt, ALU.mult).then_inc(s_v, 1)
                    nc.vector.tensor_scalar(negs[i][:], raw[i][:], nthr[:, i:i + 1], mean[:, i:i + 1],
                                            ALU.is_lt, ALU.mult).then_inc(s_v, 1)
                ve.wait_ge(s_v, 12)
                for i in range(2):
                    nc.vector.tensor_tensor(done[i], mags[i][:], negs[i][:], ALU.subtract).then_inc(s_v, 1)
                ve.wait_ge(s_v, 14)


def dense_stage(nc, sems, G, I, S, tag, heads, w_name, bias_name, out):
    width = D // heads
    with ExitStack() as ctx:
        m = Mem(nc, ctx)
        w = m.sb(f"{tag}_w", [P, 2, D])
        bias = m.sb(f"{tag}_bias", [P, D])
        att = m.sb(f"{tag}_att", [P, 2, 4, D])
        attT = m.sb(f"{tag}_attT", [P, 2, GRP])
        stat = m.sb(f"{tag}_stat", [P, 4, 6])
        mv = m.sb(f"{tag}_mv", [P, 4, 2])
        var = m.sb(f"{tag}_var", [P, 4])
        rstd = m.sb(f"{tag}_rstd", [P, 4])
        scr = m.sb(f"{tag}_scratch", [P, 4])
        dot = m.sb(f"{tag}_dot", [P, 1])
        xn = m.sb(f"{tag}_xn", [P, 4, D])
        xnT = m.sb(f"{tag}_xnT", [P, 2, 2, GRP])
        hr = m.sb(f"{tag}_relu", [P, 2, GRP])
        h = m.sb(f"{tag}_hidden", [P, 2, FC, GRP])
        psum = m.ps(f"{tag}_psum")
        X, ident, wfc, wproj = G["X"], G["ident"], G["wfc"], G["wproj"]
        src = S[tag]

        s_w = sems(f"{tag}_weights_loaded")
        s_at = [sems(f"{tag}_att_loaded{i}") for i in range(2)]
        s_out = [sems(f"{tag}_rows_written{i}") for i in range(2)]
        pe = Steps(sems(f"{tag}_pe_steps"), ["TA0", "TA1", "WO0", "WO1", "TX0", "TX1"])
        ff = Steps(sems(f"{tag}_pe_ffn"), [f"F{c}" for c in range(FC)] + ["P0", "P1"])
        act = Steps(sems(f"{tag}_act_steps"), ["TA0", "TA1", "std", "TX0", "TX1"])
        rl = Steps(sems(f"{tag}_relu_steps"), [f"F{c}" for c in range(FC)])
        sq = Steps(sems(f"{tag}_square_steps"), [f"F{c}" for c in range(FC)])
        ln = Steps(sems(f"{tag}_ln_steps"), ["add0", "add1"] + (["bias"] if bias_name else [])
                   + ["d0"] + [f"st{j}" for j in range(4)] + ["d1"] + [f"ag{j}" for j in range(4)]
                   + ["var", "rec"] + list(NEWTON) + [f"xn{j}" for j in range(4)])
        fin = Steps(sems(f"{tag}_added"), ["P0", "P1"])
        F_BANK = [2, 3, 4, 2, 3]

        def steps(front, ffn):
            def run(eng):
                front(eng, 0, 0)
                ffn(eng, 0, 0)
                ffn(eng, 1, 1)
                with eng.Fori(1, NG // 2 - 1) as i:
                    for q in range(2):
                        ffn(eng, 2 * i + q, q)
                ffn(eng, NG - 2, 0)
                ffn(eng, NG - 1, 1)
            return run

        def is_last(n):
            return isinstance(n, int) and n == NG - 1

        with nc.Block() as block:
            @block.sync
            def _(sp):
                for k in range(2):
                    sp.dma_start(w[:, k, :], I[w_name][P * k:P * k + P]).then_inc(s_w, 16)
                if bias_name:
                    sp.dma_start(bias[:], rows(I[bias_name], 0, [(0, P), (1, D)])).then_inc(s_w, 16)

                def load(b, half):
                    a = src.rearrange("(b h) p (t c) -> b p t h c", h=heads, c=width)
                    for j in range(4):
                        sp.dma_start(att[:, half, j, :].rearrange("p (h c) -> p h c", h=heads),
                                     a[bass.ds(b, 1), :, 4 * half + j].rearrange("b p h c -> p (b h) c")).then_inc(s_at[half], 16)

                def front(sp, n, q):
                    load(0, 0)

                def ffn(sp, n, q):
                    if not is_last(n):
                        wait(sp, pe.sem, pe.at(n - 1, "TA1"))
                        if isinstance(n, int):
                            load((n + 1) // 2, 1 - q)
                        else:
                            load(loop[0] + q, 1 - q)
                    if out is not None:
                        sp.wait_ge(fin.sem, fin.at(n, "P1"))
                        sp.dma_start(out[bass.ds(n * GRP, GRP), :].rearrange("(t p) c -> p t c", p=P),
                                     X[:, bass.ds(n * 4, 4), :]).then_inc(s_out[q], 16)
                loop = [None]
                front(sp, 0, 0)
                ffn(sp, 0, 0)
                ffn(sp, 1, 1)
                with sp.Fori(1, NG // 2 - 1) as i:
                    loop[0] = i
                    for q in range(2):
                        ffn(sp, 2 * i + q, q)
                ffn(sp, NG - 2, 0)
                ffn(sp, NG - 1, 1)
                if out is not None:
                    for q in range(2):
                        sp.wait_ge(s_out[q], 16 * NG // 2)

            @block.tensor
            def _(te):
                te.wait_ge(s_w, 48 if bias_name else 32)

                def turn_att(n, q, r):
                    te.wait_ge(s_at[q], 64 * (r + 1))
                    for k in range(2):
                        wait(te, ln.sem, ln.at(n - 1, f"add{k}"))
                        for j in range(4):
                            last = nc.tensor.transpose(psum[:, k, P * j:P * j + P], att[:, q, j, P * k:P * k + P], ident[:])
                        last.then_inc(pe.sem, 1)

                def project(n):
                    te.wait_ge(act.sem, act.at(n, "TA1"))
                    for i in range(2):
                        for j in range(2):
                            for k in range(2):
                                last = nc.tensor.matmul(psum[:, i, D * j:D * j + D],
                                                        attT[:, k, P * (2 * i + j):P * (2 * i + j) + P], w[:, k, :],
                                                        start=(k == 0), stop=(k == 1))
                        last.then_inc(pe.sem, 1)

                def turn_rows(n):
                    for k in range(2):
                        te.wait_ge(ln.sem, ln.at(n, "xn3"))
                        if k == 1:
                            wait(te, rl.sem, rl.at(n - 1, "F2"))
                        else:
                            wait(te, act.sem, act.at(n - 1, "TX0"))
                        for j in range(4):
                            last = nc.tensor.transpose(psum[:, (7, 4)[k], P * j:P * j + P], xn[:, j, P * k:P * k + P], ident[:])
                        last.then_inc(pe.sem, 1)

                def front(te, n, q):
                    turn_att(0, 0, 0)
                    project(0)
                    turn_rows(0)

                def ffn(te, n, q, r):
                    last_group = is_last(n)
                    if not last_group:
                        turn_att(n + 1, 1 - q, r + q)
                    te.wait_ge(act.sem, act.at(n, "TX1"))
                    for c in range(FC):
                        if c >= 3:
                            te.wait_ge(rl.sem, rl.at(n, f"F{c - 3}"))
                        elif c < 2:
                            wait(te, rl.sem, rl.at(n - 1, f"F{c + 3}"))
                        for k in range(2):
                            last = nc.tensor.matmul(psum[:, F_BANK[c], :], wfc[:, k, P * c:P * c + P], xnT[:, q, k, :],
                                                    start=(k == 0), stop=(k == 1))
                        last.then_inc(ff.sem, 1)
                    if not last_group:
                        project(n + 1)
                    te.wait_ge(sq.sem, sq.at(n, f"F{FC - 1}"))
                    for i in range(2):
                        wait(te, fin.sem, fin.at(n - 1, f"P{i}"))
                        for j in range(2):
                            for c in range(FC):
                                row = P * (2 * i + j)
                                last = nc.tensor.matmul(psum[:, 5 + i, D * j:D * j + D], h[:, q, c, row:row + P],
                                                        wproj[:, c, :], start=(c == 0), stop=(c == FC - 1))
                        last.then_inc(ff.sem, 1)
                    if not last_group:
                        turn_rows(n + 1)
                front(te, 0, 0)
                ffn(te, 0, 0, 0)
                ffn(te, 1, 1, 0)
                with te.Fori(1, NG // 2 - 1) as i:
                    for q in range(2):
                        ffn(te, 2 * i + q, q, i)
                ffn(te, NG - 2, 0, NG // 2 - 1)
                ffn(te, NG - 1, 1, NG // 2 - 1)

            @block.scalar
            def _(sc):
                def take_att(n):
                    for k in range(2):
                        sc.wait_ge(pe.sem, pe.at(n, f"TA{k}"))
                        if k == 0:
                            wait(sc, pe.sem, pe.at(n - 1, "WO1"))
                        nc.scalar.copy(attT[:, k, :], psum[:, k, :]).then_inc(act.sem, 1)

                def deviation(n):
                    sc.wait_ge(ln.sem, ln.at(n, "var"))
                    nc.scalar.activation(rstd[:], var[:], ACT.Sqrt).then_inc(act.sem, 1)

                def take_rows(n, q):
                    for k in range(2):
                        sc.wait_ge(pe.sem, pe.at(n, f"TX{k}"))
                        if k == 0:
                            wait(sc, ff.sem, ff.at(n - 2, f"F{FC - 1}"))
                        nc.scalar.copy(xnT[:, q, k, :], psum[:, (7, 4)[k], :]).then_inc(act.sem, 1)

                def front(sc, n, q):
                    take_att(0)
                    deviation(0)
                    take_rows(0, 0)

                def ffn(sc, n, q):
                    if not is_last(n):
                        take_att(n + 1)
                    for c in range(FC):
                        sc.wait_ge(ff.sem, ff.at(n, f"F{c}"))
                        wait(sc, sq.sem, sq.at(n, f"F{c}") - 2)
                        nc.scalar.activation(hr[:, (c + q) % 2, :], psum[:, F_BANK[c], :], ACT.Relu).then_inc(rl.sem, 1)
                    if not is_last(n):
                        deviation(n + 1)
                        take_rows(n + 1, 1 - q)
                steps(front, ffn)(sc)

            @block.vector
            def _(ve):
                def norm(n):
                    for i in range(2):
                        ve.wait_ge(pe.sem, pe.at(n, f"WO{i}"))
                        xs = X[:, bass.ds(n * 4 + 2 * i, 2), :]
                        nc.vector.tensor_tensor(xs, psum[:, i, :].rearrange("p (t c) -> p t c", t=2), xs,
                                                ALU.add).then_inc(ln.sem, 1)
                    ve.wait_ge(ln.sem, ln.at(n, "add1"))
                    if bias_name:
                        xs = X[:, bass.ds(n * 4, 4), :]
                        nc.vector.tensor_tensor(xs, xs, bias[:].unsqueeze(1).broadcast_to([P, 4, D]),
                                                ALU.add).then_inc(ln.sem, 1)
                        ve.wait_ge(ln.sem, ln.at(n, "bias"))
                    nc.vector.memset(dot[:], 0.0).then_inc(ln.sem, 1)
                    for j in range(4):
                        nc.vector.bn_stats(out=stat[:, j, :], in_=X[:, bass.ds(n * 4 + j, 1), :]
                                           .rearrange("p a c -> p (a c)")).then_inc(ln.sem, 1)
                    ve.wait_ge(ln.sem, ln.at(n, "st3"))
                    nc.vector.memset(dot[:], 0.0).then_inc(ln.sem, 1)
                    for j in range(4):
                        nc.vector.bn_aggr(out=mv[:, j, :], in_=stat[:, j, :]).then_inc(ln.sem, 1)
                    ve.wait_ge(ln.sem, ln.at(n, "ag3"))
                    nc.vector.tensor_scalar(var[:], mv[:, :, 1], EPS, None, ALU.add).then_inc(ln.sem, 1)
                    ve.wait_ge(act.sem, act.at(n, "std"))
                    nc.vector.reciprocal(rstd[:], rstd[:]).then_inc(ln.sem, 1)
                    before = "rec"
                    for step in NEWTON:
                        ve.wait_ge(ln.sem, ln.at(n, before))
                        newton(nc, step, rstd[:], var[:], scr[:]).then_inc(ln.sem, 1)
                        before = step
                    ve.wait_ge(ln.sem, ln.at(n, before))
                    wait(ve, pe.sem, pe.at(n - 1, "TX1"))
                    for j in range(4):
                        nc.vector.tensor_scalar(xn[:, j, :], X[:, bass.ds(n * 4 + j, 1), :].rearrange("p a c -> p (a c)"),
                                                mv[:, j, 0:1], rstd[:, j:j + 1], ALU.subtract, ALU.mult).then_inc(ln.sem, 1)

                def front(ve, n, q):
                    norm(0)

                def ffn(ve, n, q):
                    for c in range(FC):
                        ve.wait_ge(rl.sem, rl.at(n, f"F{c}"))
                        if c == 0:
                            wait(ve, ff.sem, ff.at(n - 2, "P1"))
                        nc.vector.tensor_tensor(h[:, q, c, :], hr[:, (c + q) % 2, :], hr[:, (c + q) % 2, :],
                                                ALU.mult).then_inc(sq.sem, 1)
                    if not is_last(n):
                        norm(n + 1)
                    for i in range(2):
                        ve.wait_ge(ff.sem, ff.at(n, f"P{i}"))
                        xs = X[:, bass.ds(n * 4 + 2 * i, 2), :]
                        nc.vector.tensor_tensor(xs, psum[:, 5 + i, :].rearrange("p (t c) -> p t c", t=2), xs,
                                                ALU.add).then_inc(fin.sem, 1)
                steps(front, ffn)(ve)
                ve.wait_ge(fin.sem, fin.at(NG - 1, "P1"))


def project_b(nc, sems, G, I, S):
    with ExitStack() as ctx:
        m = Mem(nc, ctx)
        wq = m.sb("pb_wq", [P, 2, 256])
        wk = m.sb("pb_wk", [P, 2, 64])
        wv = m.sb("pb_wv", [P, 2, 64])
        stat = m.sb("pb_stat", [P, TILES, 6])
        mv = m.sb("pb_mv", [P, TILES, 2])
        var = m.sb("pb_var", [P, TILES])
        rstd = m.sb("pb_rstd", [P, TILES])
        scr = m.sb("pb_scratch", [P, TILES])
        cw = m.sb("pb_cw", [P, TILES])
        xall = m.sb("pb_ln", [P, TILES, D])
        xabs = m.sb("pb_abs", [P, TILES, D])
        xn = m.sb("pb_xn", [P, 2, 4, D])
        xs = m.sb("pb_xs", [P, 2, 4, D])
        rT = m.sb("pb_rowsT", [P, 2, 4, GRP])
        split = m.sb("pb_split", [P, 2, 2, 3, GRP], BF16)
        res = m.sb("pb_res", [P, 2, 2, GRP])
        ksplit = m.sb("pb_ksplit", [64, 2, 3, GRP], BF16)
        kres = m.sb("pb_kres", [64, 2, GRP])
        psum = m.ps("pb_psum")
        X, VB_, ident = G["X"], G["VB"], G["ident"]
        s_w = sems("pb_weights_loaded")
        s_st = sems("pb_stat_steps")
        s_ln = sems("pb_ln_steps")
        s_act = sems("pb_act_ln_steps")
        pe = Steps(sems("pb_pe_steps"), ["T0", "T1", "T2", "T3", "Q0", "Q1", "K", "V"])
        act = Steps(sems("pb_act_steps"), ["T0", "T1", "T2", "T3", "h0", "h1", "hk", "V", "m0", "m1", "mk"])
        rowst = Steps(sems("pb_row_steps"), [f"{x}{j}" for x in ("xn", "xs") for j in range(4)])
        dve = Steps(sems("pb_dve_steps"), ["r0", "r1", "rk", "l0", "l1", "lk"])
        s_wr = [sems(f"pb_written{i}") for i in range(2)]
        ALL = "p t c -> p (t c)"

        def groups(body):
            def run(eng):
                body(eng, 0)
                with eng.Fori(1, B - 1) as b:
                    body(eng, b)
                body(eng, B - 1)
            return run

        with nc.Block() as block:
            @block.sync
            def _(sp):
                for k in range(2):
                    for dst, name in ((wq, "wb_q"), (wk, "wb_k"), (wv, "wb_v")):
                        sp.dma_start(dst[:, k, :], I[name][P * k:P * k + P]).then_inc(s_w, 16)

                def body(sp, b):
                    for half in range(2):
                        n, col = 2 * b + half, half * GRP
                        for f in range(2):
                            sp.wait_ge(dve.sem, dve.at(n, f"l{f}"))
                            sp.dma_start(S["qbd"][:, bass.ds(b, 1), f * P:f * P + P, col:col + GRP]
                                         .rearrange("s b p t -> p (b s) t"), split[:, half, f]).then_inc(s_wr[half], 16)
                        sp.wait_ge(dve.sem, dve.at(n, "lk"))
                        sp.dma_start(S["kbd"][:, bass.ds(b, 1), :, col:col + GRP].rearrange("s b p t -> p (b s) t"),
                                     ksplit[:, half]).then_inc(s_wr[half], 16)
                groups(body)(sp)
                for half in range(2):
                    sp.wait_ge(s_wr[half], 48 * B)

            @block.tensor
            def _(te):
                te.wait_ge(s_w, 96)

                def body(te, b):
                    for half in range(2):
                        n = 2 * b + half
                        te.wait_ge(rowst.sem, rowst.at(n, "xs3"))
                        for k in range(4):
                            wait(te, act.sem, act.at(n - 1, f"T{k}"))
                            for j in range(4):
                                last = nc.tensor.transpose(psum[:, k, P * j:P * j + P],
                                                           (xs, xn)[k // 2][:, half, j, P * (k % 2):P * (k % 2) + P],
                                                           ident[:])
                            last.then_inc(pe.sem, 1)
                        te.wait_ge(act.sem, act.at(n, "T3"))
                        for f in range(2):
                            wait(te, dve.sem, dve.at(n - 1, f"r{f}"))
                            for k in range(2):
                                last = nc.tensor.matmul(psum[:, 4 + f, :], wq[:, k, P * f:P * f + P], rT[:, half, k, :],
                                                        start=(k == 0), stop=(k == 1))
                            last.then_inc(pe.sem, 1)
                        wait(te, dve.sem, dve.at(n - 1, "rk"))
                        for k in range(2):
                            last = nc.tensor.matmul(psum[0:64, 6, :], wk[:, k, :], rT[:, half, 2 + k, :],
                                                    start=(k == 0), stop=(k == 1))
                        last.then_inc(pe.sem, 1)
                        wait(te, act.sem, act.at(n - 1, "V"))
                        for j in range(4):
                            for k in range(2):
                                last = nc.tensor.matmul(psum[:, 7, 64 * j:64 * j + 64],
                                                        rT[:, half, 2 + k, P * j:P * j + P], wv[:, k, :],
                                                        start=(k == 0), stop=(k == 1))
                        last.then_inc(pe.sem, 1)
                groups(body)(te)

            @block.scalar
            def _(sc):
                sc.wait_ge(s_ln, 1)
                nc.scalar.activation(rstd[:], var[:], ACT.Sqrt).then_inc(s_act, 1)
                sc.wait_ge(s_ln, 2 + len(NEWTON) + 2 * TILES + 1)
                nc.scalar.activation(cw[:], cw[:], ACT.Exp, scale=-1.0).then_inc(s_act, 1)

                def body(sc, b):
                    for half in range(2):
                        n = 2 * b + half
                        for k in range(4):
                            sc.wait_ge(pe.sem, pe.at(n, f"T{k}"))
                            if k == 0:
                                wait(sc, pe.sem, pe.at(n - 2, "V"))
                            nc.scalar.copy(rT[:, half, k, :], psum[:, k, :]).then_inc(act.sem, 1)
                        wait(sc, s_wr[half], 48 * b)
                        for f in range(2):
                            sc.wait_ge(pe.sem, pe.at(n, f"Q{f}"))
                            nc.scalar.copy(split[:, half, f, 0, :], psum[:, 4 + f, :]).then_inc(act.sem, 1)
                        sc.wait_ge(pe.sem, pe.at(n, "K"))
                        nc.scalar.copy(ksplit[:, half, 0, :], psum[0:64, 6, :]).then_inc(act.sem, 1)
                        sc.wait_ge(pe.sem, pe.at(n, "V"))
                        nc.scalar.copy(VB_[:, bass.ds(b * HB, HB), 4 * half:4 * half + 4, :],
                                       psum[:, 7, 0:256].rearrange("p (t h d) -> p h t d", t=4, h=HB)).then_inc(act.sem, 1)
                        for f in range(2):
                            sc.wait_ge(dve.sem, dve.at(n, f"r{f}"))
                            nc.scalar.copy(split[:, half, f, 1, :], res[:, half, f, :]).then_inc(act.sem, 1)
                        sc.wait_ge(dve.sem, dve.at(n, "rk"))
                        nc.scalar.copy(ksplit[:, half, 1, :], kres[:, half, :]).then_inc(act.sem, 1)
                groups(body)(sc)

            @block.vector
            def _(ve):
                count = [0]

                def then(op, after=True):
                    op.then_inc(s_ln, 1)
                    count[0] += 1
                    if after:
                        ve.wait_ge(s_ln, count[0])
                for t in range(TILES):
                    nc.vector.bn_stats(out=stat[:, t, :], in_=X[:, t, :]).then_inc(s_st, 1)
                for t in range(TILES):
                    ve.wait_ge(s_st, t + 1)
                    nc.vector.bn_aggr(out=mv[:, t, :], in_=stat[:, t, :]).then_inc(s_st, 1)
                ve.wait_ge(s_st, 2 * TILES)
                then(nc.vector.tensor_scalar(var[:], mv[:, :, 1], EPS, None, ALU.add))
                ve.wait_ge(s_act, 1)
                then(nc.vector.reciprocal(rstd[:], rstd[:]))
                for step in NEWTON:
                    then(newton(nc, step, rstd[:], var[:], scr[:]))
                for t in range(TILES):
                    then(nc.vector.tensor_scalar(xall[:, t, :], X[:, t, :], mv[:, t, 0:1], rstd[:, t:t + 1],
                                                 ALU.subtract, ALU.mult), t == TILES - 1)
                for t in range(TILES):
                    then(nc.vector.scalar_tensor_tensor(out=xabs[:, t, :], in0=xall[:, t, :], scalar=-1.0, in1=xall[:, t, :],
                                                        op0=ALU.mult, op1=ALU.max), t == TILES - 1)
                then(nc.vector.reduce_sum(cw[:], xabs[:], AX))
                ve.wait_ge(s_act, 2)
                then(nc.vector.tensor_scalar(cw[:], cw[:], 1.0, None, ALU.add))
                then(nc.vector.reciprocal(cw[:], cw[:]))
                then(nc.vector.memset(cw[0:64].rearrange("p (b t) -> p b t", b=B)[:, :, 0:1], 0.0))
                assert count[0] == LN_DONE

                def normalise(n, half):
                    wait(ve, pe.sem, pe.at(n - 2, "T3"))
                    for j in range(4):
                        t = bass.ds(n * 4 + j, 1)
                        nc.vector.tensor_scalar(xn[:, half, j, :], X[:, t, :].rearrange("p a c -> p (a c)"),
                                                mv[:, t, 0], rstd[:, t], ALU.subtract, ALU.mult).then_inc(rowst.sem, 1)
                    for j in range(4):
                        ve.wait_ge(rowst.sem, rowst.at(n, f"xn{j}"))
                        nc.vector.tensor_scalar(xs[:, half, j, :], xn[:, half, j, :], cw[:, bass.ds(n * 4 + j, 1)],
                                                None, ALU.mult).then_inc(rowst.sem, 1)

                normalise(0, 0)

                def body(ve, b):
                    for half in range(2):
                        n = 2 * b + half
                        if not (isinstance(n, int) and n == NG - 1):
                            normalise(n + 1, 1 - half)
                        for f in range(2):
                            ve.wait_ge(act.sem, act.at(n, f"h{f}"))
                            if f == 0:
                                wait(ve, act.sem, act.at(n - 2, "mk"))
                            nc.vector.tensor_tensor(res[:, half, f, :], psum[:, 4 + f, :], split[:, half, f, 0, :],
                                                    ALU.subtract).then_inc(dve.sem, 1)
                        ve.wait_ge(act.sem, act.at(n, "hk"))
                        nc.vector.tensor_tensor(kres[:, half, :], psum[0:64, 6, :], ksplit[:, half, 0, :],
                                                ALU.subtract).then_inc(dve.sem, 1)
                        for f in range(2):
                            ve.wait_ge(act.sem, act.at(n, f"m{f}"))
                            nc.vector.tensor_tensor(split[:, half, f, 2, :], res[:, half, f, :], split[:, half, f, 1, :],
                                                    ALU.subtract).then_inc(dve.sem, 1)
                        ve.wait_ge(act.sem, act.at(n, "mk"))
                        nc.vector.tensor_tensor(ksplit[:, half, 2, :], kres[:, half, :], ksplit[:, half, 1, :],
                                                ALU.subtract).then_inc(dve.sem, 1)
                groups(body)(ve)


LN_DONE = 2 + len(NEWTON) + 2 * TILES + 4


RB_MAX, RB_ROWS = 6 * DB, 6 * DB + 12
B_BANKS = [(qh, kt, g) for qh in range(2) for kt in range(QT) for g in range(GB)]
B_MAX = [(qt, g, kh) for qt in range(QT) for g in range(GB) for kh in range(2)]
NSB = len(B_BANKS)
B_FIRST = 9
B_OUT = ("rcp", "mul")


def b_plan(first, last):
    plan = []
    for k, qh in ([] if first else [(3, 1)]) + [(36, 0)]:
        plan += [(k, "O", qh)] + [(k + 1 + i, step, qh) for i, step in enumerate(B_OUT)]
    if not last:
        plan += [(B_FIRST + (j * (57 - B_FIRST)) // len(B_MAX), "max", j) for j in range(len(B_MAX))]
    return sorted(plan, key=lambda e: e[0])


def attention_b(nc, sems, G, I, S):
    with ExitStack() as ctx:
        m = Mem(nc, ctx)
        Q = [m.sb(f"B_Q{p}", [P, GB, N], BF16) for p in range(2)]
        Kb = [m.sb(f"B_Kb{p}", [P, N], BF16) for p in range(2)]
        Ka = [m.sb(f"B_Ka{p}", [P, N], BF16) for p in range(2)]
        V = [m.sb(f"B_V{p}", [P, QT, 32]) for p in range(2)]
        Dk = [m.sb(f"B_Dk{p}", [P, 3, GB, P], BF16) for p in range(2)]
        Dq = [m.sb(f"B_Dq{p}", [P, GB, P], BF16) for p in range(2)]
        NP = 8
        probs = m.sb("B_probs", [P, NP, GRP])
        identb = m.sb("B_identb", [P, P], BF16)
        c0 = m.sb("B_corner0", [P, 32], BF16)
        c1 = m.sb("B_corner1", [P, 32], BF16)
        mx = m.sb("B_max", [P, 2, GB, QT])
        mj = m.sb("B_max_joined", [P, GB * QT])
        mxs = m.sb("B_maxsplit", [P, 2, GB * QT], BF16)
        mT = m.sb("B_maxT", [GB * QT, 2, P], BF16)
        osb = m.sb("B_out_cols", [P, 2, GRP])
        och = m.sb("B_out_rows", [P, 2, 4 * GB, DB + 1])
        orc = m.sb("B_weights", [P, 2, 4 * GB])
        att = [m.sb(f"B_att{p}", [P, QT, GB * DB]) for p in range(2)]
        psum = m.ps("B_psum")
        ident, VBr = G["ident"], G["VB"]
        turned = psum[:, 7, :].bitcast(BF16)
        s_c = sems("b_constants_loaded")
        s_ones = sems("b_value_operands_cleared")
        s_ld = [sems(f"b_unit_loaded{p}") for p in range(2)]
        s_dk = [sems(f"b_diagonal_loaded{p}") for p in range(2)]
        s_v = sems("b_values_filled")
        s_st = sems("b_scores_ready")
        s_p = sems("b_probs_ready")
        s_pv = sems("b_probs_used")
        s_r = sems("b_ring_filled")
        s_rf = sems("b_ring_read")
        s_x = sems("b_turned_ready")
        s_xf = sems("b_turned_read")
        s_oc = sems("b_out_cols_ready")
        s_m = sems("b_max_rows_loaded")
        s_aw = [sems(f"b_out_written{p}") for p in range(2)]
        chain = Steps(sems("b_max_steps"), ["join", "hi", "lo"])
        outs = Steps(sems("b_output_steps"), [f"{s}{qh}" for qh in range(2) for s in B_OUT])
        LOADS = 11 * 16
        NMAX = len(B_MAX)
        RING = 3

        def program(block_body, unit0, tail):
            def run(eng):
                unit0(eng)
                block_body(eng, 0, 0, 0, True, False)
                with eng.Fori(0, (UB - 2) // 2) as i:
                    for p in (1, 0):
                        block_body(eng, 2 * i + (2 - p), i + (1 - p), p, False, False)
                block_body(eng, UB - 1, UB // 2 - 1, 1, False, True)
                tail(eng)
            return run

        def ring_base(u, first):
            return NMAX - 1 + (NMAX + 2) * u + int(first)

        def ring_read(u, tag, i):
            ring = [e[1:] for e in b_plan(False, False) if e[1] not in B_OUT]
            return ring_base(u, False) + ring.index((tag, i)) + 1

        def ring_bank(first):
            return (NMAX - 1 + int(first)) % RING

        with nc.Block() as block:
            @block.sync
            def _(sp):
                bf = lambda name: I[name].bitcast(BF16)
                for dst, name in ((identb, "identb"), (c0, "b_corner0"), (c1, "b_corner1")):
                    sp.dma_start(dst[:], bf(name)).then_inc(s_c, 16)
                for p in range(2):
                    sp.dma_start(Q[p][RB_ROWS:P], bf("zero_rows")[0:P - RB_ROWS]).then_inc(s_aw[p], 16)
                    sp.dma_start(Kb[p][RB_MAX:P], bf("b_kb_rows")).then_inc(s_c, 16)
                    sp.dma_start(Ka[p][RB_MAX:P], bf("b_ka_rows")).then_inc(s_c, 16)

                def load(u, p):
                    un = bass.ds(u, 1)
                    qd = S["qbd"].rearrange("s b (h d g) t -> s (b h) d (g t)", h=HB, g=GB)
                    kd = S["kbd"].rearrange("s b (h d) t -> s (b h) d t", h=HB)
                    row = 0
                    for n in (3, 2, 1):
                        sp.dma_start(Q[p][row:row + DB * n].rearrange("r g t -> r (g t)"),
                                     qd[0:n, un].rearrange("s u d x -> (s u) d x")).then_inc(s_ld[p], 16)
                        row += DB * n
                    sp.dma_start(Q[p][RB_MAX:RB_ROWS].rearrange("r g t -> r (g t)"),
                                 bf("b_q_rows")[un].rearrange("u r g t -> (u r) (g t)")).then_inc(s_ld[p], 16)
                    for K in (Kb, Ka):
                        row = 0
                        for part, reps in enumerate((3, 2, 1)):
                            sp.dma_start(K[p][row:row + DB * reps, :],
                                         kd[part, un].broadcast_to([reps, DB, N])).then_inc(s_ld[p], 16)
                            row += DB * reps
                    sp.dma_start(Dq[p][:].rearrange("p g k -> p (g k)"),
                                 bf("b_dq")[un].rearrange("u p g k -> (u p) (g k)")).then_inc(s_ld[p], 16)
                    for half in range(2):
                        lo = 64 * half
                        sp.dma_start(Dk[p][lo:lo + 64].rearrange("p s g q -> p (s g q)"),
                                     bf("b_dk")[un, lo:lo + 64].rearrange("u p s g q -> (u p) (s g q)")).then_inc(s_dk[p], 16)

                def max_rows(u, p):
                    sp.wait_ge(s_xf, u + 1)
                    for s in range(2):
                        sp.dma_start(Q[p][RB_MAX + s:RB_MAX + s + 1].rearrange("r g (t q) -> r (g t) q", q=P),
                                     mT[:, s, :]).then_inc(s_m, 16)

                def store(u, p):
                    sp.wait_ge(outs.sem, outs.at(u, "mul1"))
                    sp.dma_start(S["attb"][bass.ds(u, 1)].rearrange("u p c -> (u p) c"),
                                 att[p][:].rearrange("p t c -> p (t c)")).then_inc(s_aw[p], 16)

                def unit0(sp):
                    load(0, 0)
                    max_rows(0, 0)

                def body(sp, u, r, p, first, last):
                    if not last:
                        wait(sp, s_pv, NSB * u)
                        load(u + 1, 1 - p)
                    if not first:
                        store(u - 1, 1 - p)
                    if not last:
                        max_rows(u + 1, 1 - p)

                def tail(sp):
                    store(UB - 1, 1)
                    for p in range(2):
                        sp.wait_ge(s_aw[p], 16 * (UB // 2 + 1))
                program(body, unit0, tail)(sp)

            @block.tensor
            def _(te):
                def add(out, stationary, moving, start=False):
                    return nc.tensor.matmul(out, stationary, moving, start=start, stop=True, skip_group_check=True)

                def max_scores(p, j, out):
                    qt, g, kh = B_MAX[j]
                    q = Q[p][:, g, P * qt:P * qt + P]
                    nb = P * max(0, min(4, qt + 1 - 4 * kh))
                    if nb:
                        last = add(out[:, 0:nb], q, Kb[p][:, GRP * kh:GRP * kh + nb], True)
                    if nb < GRP:
                        last = add(out[:, nb:GRP], q, Ka[p][:, GRP * kh + nb:GRP * kh + GRP], not nb)
                    c = P * (qt - 4 * kh)
                    if 0 <= c < GRP:
                        lo = 64 if qt == 0 else 0
                        last = add(out[lo:P, c:c + P], identb[:, lo:P], Dq[p][:, g, :])
                    if 0 <= c - P < GRP:
                        last = add(out[:, c - 32:c], identb[:], c1[:])
                    if 0 <= c + P < GRP:
                        last = add(out[:, c + P:c + P + 32], identb[:], c0[:])
                    last.then_inc(s_r, 1)

                def scores(u, p, k):
                    qh, kt, g = B_BANKS[k]
                    wait(te, s_p, NSB * u + k - 1)
                    out = psum[:, 3 + k % 2, :]
                    q = Q[p][:, g, GRP * qh:GRP * qh + GRP]
                    na = P * max(0, min(4, kt - 4 * qh))
                    if na:
                        last = add(out[:, 0:na], Ka[p][:, P * kt:P * kt + P], q[:, 0:na], True)
                    if na < GRP:
                        last = add(out[:, na:GRP], Kb[p][:, P * kt:P * kt + P], q[:, na:GRP], not na)
                    c = P * (kt - 4 * qh)
                    if 0 <= c < GRP:
                        lo = 64 if kt == 0 else 0
                        for s in range(3 if g % 2 == 0 else 1):
                            last = add(out[:, c + lo:c + P], identb[:], Dk[p][:, s, g, lo:P])
                    if 0 <= c + P < GRP:
                        last = add(out[:, c + P:c + P + 32], identb[:], c0[:])
                    if 0 <= c - P < GRP:
                        last = add(out[:, c - 32:c], identb[:], c1[:])
                    last.then_inc(s_st, 1)

                def values(u, p, i):
                    qh, kt, _ = B_BANKS[4 * i]
                    te.wait_ge(s_p, NSB * u + 4 * i + 4)
                    if kt == 0:
                        wait(te, s_oc, 2 * u + qh - 1)
                    for g in range(GB):
                        last = nc.tensor.matmul(psum[32 * g:32 * g + 32, 5 + qh, :], V[p][:, kt, :],
                                                probs[:, (4 * i + g) % NP, :], start=(kt == 0), stop=True,
                                                skip_group_check=True)
                    last.then_inc(s_pv, 4)

                def turn_max(u):
                    te.wait_ge(chain.sem, chain.at(u, "lo"))
                    wait(te, s_xf, u)
                    for s in range(2):
                        last = nc.tensor.transpose(turned[0:GB * QT, P * s:P * s + P], mxs[:, s, :], identb[:])
                    last.then_inc(s_x, 1)

                def turn_output(u, qh, out):
                    te.wait_ge(s_oc, 2 * u + qh + 1)
                    for j in range(4):
                        last = nc.tensor.transpose(out[:, P * j:P * j + P], osb[:, qh, P * j:P * j + P], ident[:])
                    last.then_inc(s_r, 1)

                def unit0(te):
                    te.wait_ge(s_c, 16 * 7)
                    for p in range(2):
                        te.wait_ge(s_aw[p], 16)
                    te.wait_ge(s_ld[0], LOADS)
                    for j in range(NMAX):
                        wait(te, s_rf, j - RING + 1)
                        max_scores(0, j, psum[:, j % RING, :])
                    turn_max(0)

                def body(te, u, r, p, first, last):
                    plan = [e for e in b_plan(first, last) if e[1] not in B_OUT]
                    idx, bank = ring_base(u, first), ring_bank(first)
                    te.wait_ge(s_m, 32 * (u + 1))
                    te.wait_ge(s_v, u + 1)
                    te.wait_ge(s_dk[p], 32 * (r + 1))
                    for k in range(NSB):
                        scores(u, p, k)
                        if k % 4 == 1 and k >= 5:
                            values(u, p, (k - 5) // 4)
                        for _, tag, i in [e for e in plan if e[0] == k]:
                            wait(te, s_rf, idx - RING + 1)
                            out = psum[:, bank, :]
                            if tag == "O":
                                turn_output(u - 1 if i == 1 else u, i, out)
                            else:
                                if i == 0:
                                    te.wait_ge(s_ld[1 - p], LOADS * (r + p + 1))
                                max_scores(1 - p, i, out)
                            idx, bank = idx + 1, (bank + 1) % RING
                        if k == 59 and not last:
                            turn_max(u + 1)
                    values(u, p, NSB // 4 - 1)

                def tail(te):
                    idx = ring_base(UB - 1, False) + 2
                    wait(te, s_rf, idx - RING + 1)
                    turn_output(UB - 1, 1, psum[:, idx % RING, :])
                program(body, unit0, tail)(te)

            @block.scalar
            def _(sc):
                def take_max(u):
                    sc.wait_ge(s_x, u + 1)
                    wait(sc, s_m, 32 * u)
                    nc.scalar.copy(mT[:].rearrange("p s q -> p (s q)"), turned[0:GB * QT, 0:2 * P]).then_inc(s_xf, 1)

                def take_first_half(u, first):
                    sc.wait_ge(s_pv, NSB * u + NSB // 2)
                    if not first:
                        sc.wait_ge(s_rf, ring_read(u - 1, "O", 0))
                    nc.scalar.copy(osb[:, 0, :], psum[:, 5, :]).then_inc(s_oc, 1)

                def take_second_half(u):
                    sc.wait_ge(s_pv, NSB * (u + 1))
                    sc.wait_ge(s_rf, ring_read(u, "O", 1))
                    nc.scalar.copy(osb[:, 1, :], psum[:, 6, :]).then_inc(s_oc, 1)

                def unit0(sc):
                    take_max(0)

                def body(sc, u, r, p, first, last):
                    for k in range(NSB):
                        n = NSB * u + k
                        sc.wait_ge(s_st, n + 1)
                        wait(sc, s_pv, n - NP + 1)
                        nc.scalar.activation(probs[:, k % NP, :], psum[:, 3 + k % 2, :], ACT.Exp,
                                             scale=SCALE_B).then_inc(s_p, 1)
                        if k == 1 and not first:
                            take_second_half(u - 1)
                        if k == 34:
                            take_first_half(u, first)
                        if k == 60 and not last:
                            take_max(u + 1)

                def tail(sc):
                    take_second_half(UB - 1)
                program(body, unit0, tail)(sc)

            @block.vector
            def _(ve):
                for p in range(2):
                    nc.vector.memset(V[p][:], 0.0).then_inc(s_ones, 1)
                ve.wait_ge(s_ones, 2)
                for p in range(2):
                    nc.vector.memset(V[p][:, :, DB:DB + 1], 1.0).then_inc(s_ones, 1)

                def maximum(j, src):
                    qt, g, kh = B_MAX[j]
                    nc.vector.reduce_max(mx[:, kh, g, qt:qt + 1], src, AX).then_inc(s_rf, 1)

                def split_max(u, idx):
                    ve.wait_ge(s_rf, idx)
                    flat = "p g t -> p (g t)"
                    nc.vector.tensor_tensor(mj[:], mx[:, 0].rearrange(flat), mx[:, 1].rearrange(flat),
                                            ALU.max).then_inc(chain.sem, 1)
                    ve.wait_ge(chain.sem, chain.at(u, "join"))
                    wait(ve, s_x, u)
                    nc.vector.tensor_scalar(mxs[:, 0, :], mj[:], -1.0, None, ALU.mult).then_inc(chain.sem, 1)
                    ve.wait_ge(chain.sem, chain.at(u, "hi"))
                    nc.vector.scalar_tensor_tensor(out=mxs[:, 1, :], in0=mj[:], scalar=-1.0, in1=mxs[:, 0, :],
                                                   op0=ALU.mult, op1=ALU.subtract).then_inc(chain.sem, 1)

                def take(qh, src):
                    nc.vector.tensor_copy(och[:, qh], src.rearrange("p (x r) -> p x r", r=32)[:, :, 0:DB + 1]).then_inc(s_rf, 1)

                def output(u, r, p, qh, step, taken):
                    if step == "rcp":
                        ve.wait_ge(s_rf, taken)
                        nc.vector.reciprocal(orc[:, qh], och[:, qh, :, DB]).then_inc(outs.sem, 1)
                    else:
                        ve.wait_ge(outs.sem, outs.at(u, f"rcp{qh}"))
                        if qh == 0:
                            ve.wait_ge(s_aw[p], 16 * (r + 1))
                        nc.vector.tensor_tensor(att[p][:, 4 * qh:4 * qh + 4, :].rearrange("p t (g d) -> p (t g) d", g=GB),
                                                och[:, qh, :, 0:DB],
                                                orc[:, qh].unsqueeze(2).broadcast_to([P, 4 * GB, DB]),
                                                ALU.mult).then_inc(outs.sem, 1)

                def unit0(ve):
                    for j in range(NMAX):
                        ve.wait_ge(s_r, j + 1)
                        maximum(j, psum[:, j % RING, :])
                    split_max(0, NMAX)

                def body(ve, u, r, p, first, last):
                    idx, bank = ring_base(u, first), ring_bank(first)
                    for _, tag, i in b_plan(first, last):
                        if tag != "max":
                            out_u, out_r, out_p = (u - 1, r - 1 + p, 1 - p) if i == 1 else (u, r, p)
                        if tag in B_OUT:
                            output(out_u, out_r, out_p, i, tag, taken)
                            continue
                        ve.wait_ge(s_r, idx + 1)
                        src = psum[:, bank, :]
                        if tag == "O":
                            take(i, src)
                            taken = idx + 1
                        else:
                            maximum(i, src)
                            if i == NMAX - 1:
                                split_max(u + 1, idx + 1)
                        idx, bank = idx + 1, (bank + 1) % RING

                def tail(ve):
                    idx = ring_base(UB - 1, False) + 2
                    ve.wait_ge(s_r, idx + 1)
                    take(1, psum[:, idx % RING, :])
                    for step in B_OUT:
                        output(UB - 1, UB // 2 - 1, 1, 1, step, idx + 1)
                program(body, unit0, tail)(ve)

            @block.gpsimd
            def _(po):
                po.wait_ge(s_ones, 4)

                def fill(u, p):
                    nc.gpsimd.tensor_copy(V[p][:, :, 0:DB], VBr[:, bass.ds(u, 1)].rearrange("p u t d -> p (u t) d")
                                          ).then_inc(s_v, 1)

                def body(po, u, r, p, first, last):
                    if not last:
                        wait(po, s_pv, NSB * u)
                        fill(u + 1, 1 - p)
                program(body, lambda po: fill(0, 0), lambda po: None)(po)


def build(nc, I, out):
    def dram(name, shape, dt):
        return nc.dram_tensor(name, shape, dt, kind="Internal").ap()

    S = {
        "qd": dram("qd", (6, B, 256, N), BF16),
        "kd": dram("kd", (3, B, 64, N), BF16),
        "vkd": dram("vkd", (B * N, P), F32),
        "ckd": dram("ckd", (3, DA, UA, NBLK), BF16),
        "att": dram("att", (UA, P, QT * GA * DA), F32),
        "qbd": dram("qbd", (3, B, 256, N), BF16),
        "kbd": dram("kbd", (3, B, 64, N), BF16),
        "attb": dram("attb", (UB, P, QT * GB * DB), F32),
        "cvd": dram("cvd", (UA, NBLK, DA), F32),
    }
    with ExitStack() as ctx:
        m = Mem(nc, ctx)
        G = {
            "X": m.sb("X", [P, TILES, D]),
            "ident": m.sb("ident_f32", [P, P]),
        }
        with ExitStack() as actx:
            ma = Mem(nc, actx)
            G["GT"] = ma.sb("GT", [P, UA, QT, 12])
            G["VT"] = ma.sb("VT", [P, B, HA, QT, DA])
            G["VS"] = ma.sb("VS", [P, B, HA, QT, DA])
            project_a(nc, m.sem, G, I, S)
            compress_a(nc, m.sem, G, I, S)
            attention_a(nc, m.sem, G, I, S)
        G["wfc"] = m.sb("wfc", [P, 2, HID])
        G["wproj"] = m.sb("wproj", [P, FC, D])
        ternarize(nc, m.sem, G, I)
        dense_stage(nc, m.sem, G, I, S, "att", HA, "w_out", None, None)
        with ExitStack() as bctx:
            G["VB"] = Mem(nc, bctx).sb("VB", [P, UB, QT, DB])
            project_b(nc, m.sem, G, I, S)
            attention_b(nc, m.sem, G, I, S)
        dense_stage(nc, m.sem, G, I, S, "attb", HB, "w_o", "b_o", out)


def constants():
    import numpy as np

    c = {"ident": np.eye(P, dtype=np.float32)}
    inv = (np.float32(1.0) / np.float32(10000.0) ** (np.arange(0, DA, 2, dtype=np.float32) / np.float32(DA))).astype(np.float32)
    ang = np.arange(N, dtype=np.float32)[:, None] * inv[None, :]
    cos, sin = np.cos(ang), np.sin(ang)
    for name, of in (("rope_q", (np.arange(P) // GA) % DA), ("rope_k", np.arange(64) % DA)):
        sign = np.where(of % 2 == 0, -1.0, 1.0).astype(np.float32)
        c[name] = np.ascontiguousarray(np.stack([cos[:, of // 2].T, sin[:, of // 2].T * sign[:, None]], 1), dtype=np.float32)

    def bits(a):
        return (np.ascontiguousarray(a, dtype=np.float32).view(np.uint32) >> 16).astype(np.uint16)

    q, k = np.arange(P)[:, None], np.arange(P)[None, :]
    c["identb"] = bits(np.eye(P))
    c["causal_q"] = bits(np.where(k > q, NEG, 0.0))
    c["causal_k"] = bits(np.where(q > k, NEG, 0.0))
    rel = np.arange(192)[None, :]
    band = (rel >= q) & (rel <= q + WIN)
    c["band_q"] = bits(np.where(np.stack([band & (rel >= WIN), band], 1), 0.0, NEG))
    i = np.arange(WIN)[None, :]
    band = (q >= i) & (q <= i + WIN)
    c["band_k"] = bits(np.where(np.stack([band & (q >= WIN), band], 1), 0.0, NEG))
    t, j, n = np.arange(QT)[None, :, None], np.arange(NBLK)[None, None, :], np.arange(N)
    c["own"] = (j == (P * t + np.arange(P)[:, None, None]) // BLK).astype(np.float32)
    seen = (np.arange(NBLK)[:, None] == NBLK - 1) | (BLK * (np.arange(NBLK)[:, None] + 1) - 1 < n[None, :])
    qc = np.zeros((P - R_MAX, GA, N), np.float32)
    qc[R_BLK - R_MAX:] = np.where(seen, 0.0, NEG)[:, None, :]
    c["qc_rows"] = bits(qc)
    c["zero_rows"] = bits(np.zeros((P - R_MAX, GA, N)))
    kf = np.zeros((P - R_MAX, PAD + N), np.float32)
    kf[0:2] = 1.0
    kf[R_BLK - R_MAX:, PAD:] = np.arange(NBLK)[:, None] == n[None, :] // BLK
    c["kf_rows"] = bits(kf)
    kw = np.zeros((P - R_MAX, PAD + N), np.float32)
    kw[2:4] = 1.0
    c["kw_rows"] = bits(kw)
    kc = np.zeros((P - R_MAX, NBLK), np.float32)
    kc[0:2] = 1.0
    kc[R_BLK - R_MAX:] = np.eye(NBLK)
    c["kc_rows"] = bits(kc)

    def parts(a):
        out, rest = [], np.asarray(a, np.float32)
        for _ in range(3):
            u = rest.view(np.uint32)
            hi = ((u + 0x7FFF + ((u >> 16) & 1)) & 0xFFFF0000).view(np.float32)
            out.append(hi)
            rest = rest - hi
        return out

    slopes = np.float32(2.0 ** -0.5) ** np.arange(1, HB * GB + 1, dtype=np.float32)
    s4 = (slopes / np.float32(SCALE_B)).astype(np.float32).reshape(HB, GB)
    live = n >= 64
    rq = np.zeros((HB, 12, GB, N), np.float32)
    for i, part in enumerate(parts(s4[:, :, None] * n.astype(np.float32))):
        rq[:, 2 + i] = part * live
    for i, part in enumerate(parts(s4)):
        rq[:, 5 + i] = rq[:, 8 + i] = part[:, :, None] * live
    rq[:, 11] = NEG * live
    c["b_q_rows"] = np.tile(bits(rq), (B, 1, 1, 1))
    for name, sign in (("b_kb_rows", 1.0), ("b_ka_rows", -1.0)):
        k = np.zeros((P - RB_MAX, N), np.float32)
        k[0:2] = 1.0
        k[2:5] = -sign
        k[5:8], k[8:11] = sign * (n // 8 * 8), sign * (n % 8)
        k[11] = n < 64
        c[name] = bits(k)
    row, col = np.arange(P)[:, None], np.arange(P)[None, :]
    full = -2.0 * s4[..., None, None] * np.maximum(row - col, 0)
    dk = parts(full.astype(np.float32))
    band = np.abs(row - col) <= 32
    dk = [np.where(band, NEG if i == 0 else 0.0, x) for i, x in enumerate(dk)]
    c["b_dk"] = np.tile(bits(np.stack(dk, 0).transpose(1, 3, 0, 2, 4)), (B, 1, 1, 1, 1))
    c["b_dq"] = np.tile(bits(dk[0].transpose(0, 3, 1, 2)), (B, 1, 1, 1))
    edge, cc = np.arange(P)[:, None], np.arange(32)[None, :]
    c["b_corner0"] = bits(np.where(edge >= 96 + cc, NEG, 0.0))
    c["b_corner1"] = bits(np.where(edge <= cc, NEG, 0.0))
    return c



def layout(inputs):
    import numpy as np
    a = {k.removeprefix("L0_"): np.asarray(v) for k, v in inputs.items()}
    wqkv = a["attn_a_w_qkv"]
    q, k, v = wqkv[:, :256].reshape(D, HA, GA, DA), wqkv[:, 256:320].reshape(D, HA, DA), wqkv[:, 320:384]
    swap = np.arange(DA) ^ 1
    d = {"x": a["attn_a_hidden_states"].reshape(B * N, D)}
    plain = q.transpose(0, 1, 3, 2)
    d["w_q"] = np.stack([plain.reshape(D, 256), plain[:, :, swap].reshape(D, 256)], 1)
    d["w_k"] = np.stack([k.reshape(D, 64), k[:, :, swap].reshape(D, 64)], 1)
    d["w_tok"] = np.concatenate([a["attn_a_w_gate"], v, wqkv[:, 256:320]], 1)
    d["b_gate"] = a["attn_a_b_gate"].reshape(1, 96)
    for kind in "kv":
        d[f"{kind}_cw1"] = a[f"attn_a_{kind}_cw1"]
        d[f"{kind}_cw2"] = a[f"attn_a_{kind}_cw2"]
        d[f"{kind}_pos"] = a[f"attn_a_{kind}_pos"].reshape(HA, P).T
        d[f"{kind}_cb1"] = a[f"attn_a_{kind}_cb1"].reshape(P, 1)
    d["k_cb2"] = a["attn_a_k_cb2"].reshape(DA, 1)
    d["v_cb2"] = a["attn_a_v_cb2"].reshape(1, DA)
    d["mem_ck"] = a["attn_a_mem_ck"].reshape(HA, DA).T
    d["mem_cv"] = a["attn_a_mem_cv"].reshape(HA, DA)
    d["w_out"] = a["attn_a_w_out"]
    d["w_fc"], d["w_proj"] = a["ffn_w_fc"].T, a["ffn_w_proj"].T
    d["wb_q"] = a["attn_b_Wq"].reshape(D, HB, GB, DB).transpose(0, 1, 3, 2).reshape(D, 256)
    d["wb_k"], d["wb_v"] = a["attn_b_Wkv"][:, :64], a["attn_b_Wkv"][:, 64:]
    d["w_o"], d["b_o"] = a["attn_b_Wo"], a["attn_b_bo"].reshape(1, D)
    return d


def kernel(**inputs):
    import numpy as np
    import concourse.bacc as bacc
    from concourse.bass_utils import run_bass_kernel_spmd

    nc = bacc.Bacc("TRN2", target_bir_lowering=False, num_devices=1)
    arrays = {f"in_{k}": np.ascontiguousarray(v) for k, v in {**layout(inputs), **constants()}.items()}
    I = {k[3:]: nc.dram_tensor(k, v.shape, mybir.dt.from_np(v.dtype), kind="ExternalInput").ap()
         for k, v in arrays.items()}
    out = nc.dram_tensor("out", (B * N, D), F32, kind="ExternalOutput").ap()
    build(nc, I, out)
    r = run_bass_kernel_spmd(nc, [arrays], core_ids=[0])
    return r.results[0]["out"].reshape(B, N, D)
```
